# Optimizing a Trainium2 kernel written in Bass

```python
import numpy as np
import jax
import jax.numpy as jnp

def _softmax(x, axis=-1):
    return jax.nn.softmax(x, axis=axis)

def _gelu(x):
    return jax.nn.gelu(x, approximate=True)

def _silu(x):
    return jax.nn.silu(x)

def _sigmoid(x):
    return jax.nn.sigmoid(x)

def _layernorm(x, axis=-1, eps=1e-05):
    m = jnp.mean(x, axis=axis, keepdims=True)
    v = jnp.var(x, axis=axis, keepdims=True)
    return (x - m) / jnp.sqrt(v + eps)

def _scatter_add(tgt, idx, src, axis=0):
    return tgt.at[idx].add(src)

def _segment_sum(src, seg, n):
    return jax.ops.segment_sum(src, seg, n)
kernel_name = 'mk_adj_ffn_d1_adj_r2_147eda'

def setup_inputs(seed: int=0):
    np.random.seed(seed)
    _w = jnp.asarray

    def _rec_inputs():
        import jax
        import jax.numpy as jnp
        _gk = jax.random.key(seed)
        x = -0.0002928 + 1 * jax.random.normal(jax.random.fold_in(_gk, 1), (8, 2048, 128), jnp.float32)
        _a = jax.random.bernoulli(jax.random.fold_in(_gk, 2), 0.0078125, (8, 2048, 2048))
        _a = jnp.logical_or(_a, jnp.swapaxes(_a, -1, -2))
        _a = jnp.logical_or(_a, jnp.eye(2048, dtype=bool))
        _af = _a.astype(jnp.float32)
        _af = _af * jax.random.uniform(jax.random.fold_in(_gk, 3), (8, 2048, 2048), jnp.float32, 0.05, 1)
        adj = _af
        return (x, adj)
    x, adj = _rec_inputs()

    def _L0_gnn_setup():
        import jax, jax.numpy as jnp
        import numpy as np
        ALPHA = 0.2
        MLP_ALPHA = 0.01
        EPS = 1e-05

        def leaky(x, a):
            return jnp.where(x >= 0, x, a * x)
        key = jax.random.key(seed)
        ks = jax.random.split(key, 12)
        B, N, FIN, FOUT, K = (4, 2048, 128, 128, 64)
        s = 0.05
        return {'h': jax.random.normal(ks[0], (B, N, FIN), jnp.float32), 'adj': jax.random.uniform(ks[1], (B, N, N), jnp.float32), 'W': jax.random.normal(ks[2], (FIN, FOUT), jnp.float32) * s, 'a': jax.random.normal(ks[3], (FOUT, 1), jnp.float32) * s, 'ln_g': jnp.ones((FOUT,), jnp.float32), 'ln_b': jnp.zeros((FOUT,), jnp.float32), 'W1': jax.random.normal(ks[4], (FOUT, FOUT), jnp.float32) * s, 'b1': jnp.zeros((FOUT,), jnp.float32), 'W2': jax.random.normal(ks[5], (FOUT, FOUT), jnp.float32) * s, 'b2': jnp.zeros((FOUT,), jnp.float32), 'W3': jax.random.normal(ks[6], (FOUT, FOUT), jnp.float32) * s, 'b3': jnp.zeros((FOUT,), jnp.float32), 'k': K}
    _L0_gnn_all = _L0_gnn_setup()
    _L0_gnn_in = {k: v for k, v in _L0_gnn_all.items() if k in ('W', 'a', 'ln_g', 'ln_b', 'W1', 'b1', 'W2', 'b2', 'W3', 'b3')}
    del _L0_gnn_all

    def _L0_ffn_setup():
        import jax, jax.numpy as jnp
        import numpy as np
        BN_EPS = 0.001

        def _bn(h, g, b, m, v):
            return g * (h - m) * jax.lax.rsqrt(v + BN_EPS) + b
        key = jax.random.key(seed)
        ks = jax.random.split(key, 8)
        B, F, Df = (128, 64, 128)
        E, H, D = (8, 128, 128)
        s1 = 1.0 / np.sqrt(Df)
        s2 = 1.0 / np.sqrt(H)
        return {'x': jax.random.normal(ks[0], (B, F, Df), jnp.float32), 'Wr': jax.random.normal(ks[1], (Df, E), jnp.float32) * s1, 'br': jnp.zeros((E,), jnp.float32), 'W1': jax.random.normal(ks[2], (E, Df, H), jnp.float32) * s1, 'b1': jnp.zeros((E, H), jnp.float32), 'g1': jnp.ones((E, H), jnp.float32), 'be1': jnp.zeros((E, H), jnp.float32), 'm1': jnp.zeros((E, H), jnp.float32), 'v1': jnp.ones((E, H), jnp.float32), 'W2': jax.random.normal(ks[3], (E, H, H), jnp.float32) * s2, 'b2': jnp.zeros((E, H), jnp.float32), 'g2': jnp.ones((E, H), jnp.float32), 'be2': jnp.zeros((E, H), jnp.float32), 'm2': jnp.zeros((E, H), jnp.float32), 'v2': jnp.ones((E, H), jnp.float32), 'Wo': jax.random.normal(ks[4], (E, H, D), jnp.float32) * s2, 'bo': jnp.zeros((E, D), jnp.float32)}
    _L0_ffn_all = _L0_ffn_setup()
    _L0_ffn_in = {k: v for k, v in _L0_ffn_all.items() if k in ('Wr', 'br', 'W1', 'b1', 'g1', 'be1', 'm1', 'v1', 'W2', 'b2', 'g2', 'be2', 'm2', 'v2', 'Wo', 'bo')}
    del _L0_ffn_all
    return {'x': x, 'adj': adj, 'L0_gnn_W': _L0_gnn_in['W'], 'L0_gnn_a': _L0_gnn_in['a'], 'L0_gnn_ln_g': _L0_gnn_in['ln_g'], 'L0_gnn_ln_b': _L0_gnn_in['ln_b'], 'L0_gnn_W1': _L0_gnn_in['W1'], 'L0_gnn_b1': _L0_gnn_in['b1'], 'L0_gnn_W2': _L0_gnn_in['W2'], 'L0_gnn_b2': _L0_gnn_in['b2'], 'L0_gnn_W3': _L0_gnn_in['W3'], 'L0_gnn_b3': _L0_gnn_in['b3'], 'L0_ffn_Wr': _L0_ffn_in['Wr'], 'L0_ffn_br': _L0_ffn_in['br'], 'L0_ffn_W1': _L0_ffn_in['W1'], 'L0_ffn_b1': _L0_ffn_in['b1'], 'L0_ffn_g1': _L0_ffn_in['g1'], 'L0_ffn_be1': _L0_ffn_in['be1'], 'L0_ffn_m1': _L0_ffn_in['m1'], 'L0_ffn_v1': _L0_ffn_in['v1'], 'L0_ffn_W2': _L0_ffn_in['W2'], 'L0_ffn_b2': _L0_ffn_in['b2'], 'L0_ffn_g2': _L0_ffn_in['g2'], 'L0_ffn_be2': _L0_ffn_in['be2'], 'L0_ffn_m2': _L0_ffn_in['m2'], 'L0_ffn_v2': _L0_ffn_in['v2'], 'L0_ffn_Wo': _L0_ffn_in['Wo'], 'L0_ffn_bo': _L0_ffn_in['bo']}

def reference(x, adj, L0_gnn_W, L0_gnn_a, L0_gnn_ln_g, L0_gnn_ln_b, L0_gnn_W1, L0_gnn_b1, L0_gnn_W2, L0_gnn_b2, L0_gnn_W3, L0_gnn_b3, L0_ffn_Wr, L0_ffn_br, L0_ffn_W1, L0_ffn_b1, L0_ffn_g1, L0_ffn_be1, L0_ffn_m1, L0_ffn_v1, L0_ffn_W2, L0_ffn_b2, L0_ffn_g2, L0_ffn_be2, L0_ffn_m2, L0_ffn_v2, L0_ffn_Wo, L0_ffn_bo):
    import jax
    import jax.numpy as jnp

    def _L0_gnn_ref(h, adj, W, a, ln_g, ln_b, W1, b1, W2, b2, W3, b3, k):
        import jax, jax.numpy as jnp
        import numpy as np
        ALPHA = 0.2
        MLP_ALPHA = 0.01
        EPS = 1e-05

        def leaky(x, a):
            return jnp.where(x >= 0, x, a * x)
        Wh = h @ W
        B, N, Fd = Wh.shape
        C = N // k
        Whc = Wh.reshape(B, C, k, Fd)
        e = leaky(jnp.squeeze(Whc @ a, -1), ALPHA)
        idx = jnp.arange(C)
        blocks = adj.reshape(B, C, k, C, k)[:, idx, :, idx, :]
        blocks = jnp.transpose(blocks, (1, 0, 2, 3))
        scores = jax.nn.softmax(blocks * e[..., :, None], axis=-1)
        out = jnp.einsum('bcij,bcjf->bcif', scores, Whc)
        y = leaky(out @ W1 + b1, MLP_ALPHA)
        y = leaky(y @ W2 + b2, MLP_ALPHA)
        y = y @ W3 + b3
        z = y + out
        mu = jnp.mean(z, axis=-1, keepdims=True)
        var = jnp.var(z, axis=-1, keepdims=True)
        z = (z - mu) / jnp.sqrt(var + EPS) * ln_g + ln_b
        return z.reshape(B, N, Fd)

    def _L0_ffn_ref(x, Wr, br, W1, b1, g1, be1, m1, v1, W2, b2, g2, be2, m2, v2, Wo, bo):
        import jax, jax.numpy as jnp
        import numpy as np
        BN_EPS = 0.001

        def _bn(h, g, b, m, v):
            return g * (h - m) * jax.lax.rsqrt(v + BN_EPS) + b
        feat = jnp.mean(x, axis=0)
        w = jax.nn.softmax(feat @ Wr + br, axis=-1)
        h = jnp.einsum('bfd,edh->bfeh', x, W1) + b1
        h = jax.nn.relu(_bn(h, g1, be1, m1, v1))
        h = jnp.einsum('bfeh,ehk->bfek', h, W2) + b2
        h = jax.nn.relu(_bn(h, g2, be2, m2, v2))
        y = jnp.einsum('bfeh,ehd->bfed', h, Wo) + bo
        return jnp.einsum('bfed,fe->bfd', y, w)
    x = x + _L0_gnn_ref(_layernorm(x, axis=-1), adj, L0_gnn_W, L0_gnn_a, L0_gnn_ln_g, L0_gnn_ln_b, L0_gnn_W1, L0_gnn_b1, L0_gnn_W2, L0_gnn_b2, L0_gnn_W3, L0_gnn_b3, 64)
    x = x + _L0_ffn_ref(_layernorm(x, axis=-1), L0_ffn_Wr, L0_ffn_br, L0_ffn_W1, L0_ffn_b1, L0_ffn_g1, L0_ffn_be1, L0_ffn_m1, L0_ffn_v1, L0_ffn_W2, L0_ffn_b2, L0_ffn_g2, L0_ffn_be2, L0_ffn_m2, L0_ffn_v2, L0_ffn_Wo, L0_ffn_bo)
    return x

_drawn_inputs = setup_inputs


def setup_inputs(seed=0):
    import zlib

    import numpy as np

    out = dict(_drawn_inputs(seed))
    spreads = {'L0_gnn_ln_g': (1.0, 0.2),
     'L0_gnn_ln_b': (0.0, 0.1),
     'L0_gnn_b1': (0.0, 0.1),
     'L0_gnn_b2': (0.0, 0.1),
     'L0_gnn_b3': (0.0, 0.1),
     'L0_ffn_br': (0.0, 0.1),
     'L0_ffn_b1': (0.0, 0.52),
     'L0_ffn_g1': (1.0, 0.2),
     'L0_ffn_be1': (0.0, 0.526),
     'L0_ffn_m1': (0.0, 0.499),
     'L0_ffn_v1': (1.0, 0.6),
     'L0_ffn_b2': (0.0, 0.359),
     'L0_ffn_g2': (1.0, 0.2),
     'L0_ffn_be2': (0.0, 0.372),
     'L0_ffn_m2': (0.0, 0.392),
     'L0_ffn_v2': (1.0, 0.6),
     'L0_ffn_bo': (0.0, 0.275)}
    factors = {'adj': 5.559, 'L0_gnn_a': 5.317}
    for name, (base, spread) in spreads.items():
        noise = np.random.default_rng([zlib.crc32(name.encode()), seed]).standard_normal(out[name].shape)
        drawn = base * np.exp(spread * noise) if base else spread * noise
        out[name] = jnp.asarray(drawn.astype(out[name].dtype))
    for name, factor in factors.items():
        out[name] = (out[name] * factor).astype(out[name].dtype)
    return out
```

```python
from contextlib import ExitStack

import concourse.bass as bass
from concourse import mybir

ALU = mybir.AluOpType
ACT = mybir.ActivationFunctionType
AX = mybir.AxisListType.X
F32 = mybir.dt.float32
F16 = mybir.dt.float16

P = 128
ALPHA = 0.2
MLP_ALPHA = 0.01
LN_EPS = 1e-5
BN_EPS = 1e-3
X_BOUND = 11.4
K1 = 2.0 ** 8
K2 = 2.0 ** 14
K3 = 2.0 ** 13


def build(nc, x, adj, W, a, ln_g, ln_b, W1, b1, W2, b2, W3, b3, Wr, br,
          E1, c1, g1, be1, m1, v1, E2, c2, g2, be2, m2, v2, Eo, bo, out):
    NB, S, D = x.shape
    NE = E1.shape[0]
    C = 64
    T = S // P
    N = NB * P
    HALF = N // 2
    assert D == P and HALF == 512 and T % 2 == 0 and NE == 8

    x_t = x.rearrange("b (t p) d -> t p b d", p=P)
    out_t = out.rearrange("b (t p) d -> t p b d", p=P)
    adj_t = adj.rearrange("b (t k i) (u l j) -> t k u l i b j", k=2, i=C, l=2, j=C)

    with ExitStack() as ctx:
        def sb(name, shape, dt=F32):
            return ctx.enter_context(nc.sbuf_tensor(name, shape, dt))

        def psum(name, shape):
            return ctx.enter_context(nc.psum_tensor(name, shape, F32))

        def sem(name):
            return ctx.enter_context(nc.semaphore(name))

        ident = sb("ident", [P, P])
        ones = sb("ones", [P, P])
        bound_x = sb("bound_x", [P, P])
        bound_h = sb("bound_h", [P, P])
        bound_o = sb("bound_o", [P, P])
        inv_k1 = sb("inv_k1", [NE, P])
        inv_k2 = sb("inv_k2", [NE, P])
        neg_half = sb("neg_half", [P, 256])
        same_e = sb("same_e", [P, NE * NE])
        pick = sb("pick", [2 * NE, NE])
        spread = sb("spread", [2 * NE, NE, P], F16)
        w_sb = sb("w_sb", [P, P])
        w1_sb = sb("w1_sb", [P, P])
        w2_sb = sb("w2_sb", [P, P])
        w3_sb = sb("w3_sb", [P, P])
        wt_sb = sb("wt_sb", [P, P])
        a_col = sb("a_col", [P, 1])
        a_wide = sb("a_wide", [P, P])
        wa_wide = sb("wa_wide", [P, P])
        b1_col = sb("b1_col", [P, 1])
        b2_col = sb("b2_col", [P, 1])
        b3_col = sb("b3_col", [P, 1])
        lng = sb("lng", [P, P])
        lnb = sb("lnb", [P, P])
        wr_sb = sb("wr_sb", [P, NE])
        br_sb = sb("br_sb", [P, NE])
        e1_hi = sb("e1_hi", [P, NE, P], F16)
        e1_lo = sb("e1_lo", [P, NE, P], F16)
        e2_hi = sb("e2_hi", [P, NE, P], F16)
        e2_lo = sb("e2_lo", [P, NE, P], F16)
        eo_hi = sb("eo_hi", [P, NE, P], F16)
        eo_lo = sb("eo_lo", [P, NE, P], F16)
        bo_row = sb("bo_row", [NE, P])
        bn_g = sb("bn_g", [NE, 2, P])
        bn_v = sb("bn_v", [NE, 2, P])
        bn_m = sb("bn_m", [NE, 2, P])
        bn_b = sb("bn_b", [NE, 2, P])
        bn_c = sb("bn_c", [NE, 2, P])
        bn_s = sb("bn_s", [NE, 2, P])
        bn_t = sb("bn_t", [NE, 2, P])
        bn_abs = sb("bn_abs", [NE, 2, P])
        s_diag = sb("s_diag", [NE, 2, NE, P])
        t_diag = sb("t_diag", [NE, 2, NE, P])
        t_col = sb("t_col", [P, 2, NE])
        t2_diag = sb("t2_diag", [P, NE, NE])
        u_col = sb("u_col", [P, 2, NE])
        iu_col = sb("iu_col", [P, 2, NE])
        bias1 = sb("bias1", [P, NE])
        neg_bias2 = sb("neg_bias2", [P, NE])
        uo_wide = sb("uo_wide", [P, P])
        iuo_col = sb("iuo_col", [P, 1])
        c_row = sb("c_row", [NE, P])
        x_in = [sb(f"x_in{i}", [P, NB, P]) for i in range(2)]
        adj_in = [sb(f"adj_in{i}", [P, NB, C]) for i in range(2)]
        stat_a = sb("stat_a", [P, NB, 6])
        mean2_a = sb("mean2_a", [P, NB])
        gap_a = sb("gap_a", [P, NB])
        ve_a = sb("ve_a", [P, NB])
        rstd_a = sb("rstd_a", [P, NB])
        shift_a = sb("shift_a", [P, NB])
        xn = sb("xn", [P, NB, P])
        xn_t = sb("xn_t", [P, N])
        xn_wa = sb("xn_wa", [P, NB, P])
        factor = sb("factor", [P, NB])
        scores = sb("scores", [P, NB, C])
        top = sb("top", [P, NB])
        total = sb("total", [P, NB])
        inv_total = sb("inv_total", [P, NB])
        probs = [sb(f"probs{i}", [P, NB, 2, C]) for i in range(2)]
        wh = [sb(f"wh{i}", [P, NB, P]) for i in range(2)]
        probs_t = sb("probs_t", [P, NB, P])
        att = sb("att", [P, N])
        mlp1 = sb("mlp1", [P, N])
        mlp2 = sb("mlp2", [P, N])
        z_t = sb("z_t", [P, N])
        z = sb("z", [P, NB, P])
        stat_b = sb("stat_b", [P, NB, 6])
        mean2_b = sb("mean2_b", [P, NB])
        gap_b = sb("gap_b", [P, NB])
        ve_b = sb("ve_b", [P, NB])
        rstd_b = sb("rstd_b", [P, NB])
        shift_b = sb("shift_b", [P, NB])
        xb = sb("xb", [P, NB, P])
        x1 = [sb(f"x1_{i}", [P, NB, P]) for i in range(2)]
        stat_c = sb("stat_c", [P, NB, 6])
        mean2_c = sb("mean2_c", [P, NB])
        gap_c = sb("gap_c", [P, NB])
        ve_c = sb("ve_c", [P, NB])
        rstd_c = sb("rstd_c", [P, NB])
        shift_c = sb("shift_c", [P, NB])
        x1n = sb("x1n", [P, NB, P])
        sum4 = sb("sum4", [P, 4, P])
        sum2 = sb("sum2", [P, 2, P])
        feat = sb("feat", [P, P])
        feat_t = sb("feat_t", [P, P])
        logit = sb("logit", [P, NE])
        neg_top = sb("neg_top", [P, 1])
        ex = sb("ex", [P, NE])
        ex_sum = sb("ex_sum", [P, 1])
        ex_inv = sb("ex_inv", [P, 1])
        rw = sb("rw", [P, NE])
        rw16 = sb("rw16", [P, 2 * NE], F16)
        ident16 = sb("ident16", [P, P], F16)
        rw_t = sb("rw_t", [NE, P])
        rw16_t = sb("rw16_t", [2 * NE, P], F16)
        x_hi = [sb(f"x_hi{i}", [P, N], F16) for i in range(2)]
        x_lo = [sb(f"x_lo{i}", [P, N], F16) for i in range(2)]
        route = [sb(f"route{i}", [P, NE, P]) for i in range(2)]
        y_bias = sb("y_bias", [P, P])
        x1_kept = [sb(f"x1_kept{i}", [P, NB, P]) for i in range(2)]
        r1 = [sb(f"r1_{i}", [P, N]) for i in range(2)]
        h1_hi = [sb(f"h1_hi{i}", [P, N], F16) for i in range(2)]
        h1_lo = [sb(f"h1_lo{i}", [P, N], F16) for i in range(2)]
        h2_hi = [sb(f"h2_hi{i}", [P, N], F16) for i in range(2)]
        h2_lo = [sb(f"h2_lo{i}", [P, N], F16) for i in range(2)]
        y_t = sb("y_t", [P, N])
        y_out = [sb(f"y_out{i}", [P, NB, P]) for i in range(2)]
        e1_sb = r1[0][:, :].rearrange("p (e h) -> p e h", e=NE)
        e2_sb = r1[1][:, :].rearrange("p (e h) -> p e h", e=NE)
        eo_sb = y_t[:, :].rearrange("p (e h) -> p e h", e=NE)
        abs_w, u_wide = y_out
        Z1 = psum("Z1", [P, N])
        Z2 = psum("Z2", [P, N])
        Y = psum("Y", [P, N])
        F = psum("F", [P, N])

        gnn_landed = sem("gnn_landed")
        ffn_landed = sem("ffn_landed")
        ident_zero = sem("ident_zero")
        ident_ready = sem("ident_ready")
        consts_ready = sem("consts_ready")
        same_zero = sem("same_zero")
        same_ready = sem("same_ready")
        probs_zero = sem("probs_zero")
        wt_done = sem("wt_done")
        wt_ready = sem("wt_ready")
        wa_done = sem("wa_done")
        a_wide_ready = sem("a_wide_ready")
        wa_ready = sem("wa_ready")
        pick_ready = sem("pick_ready")
        spread_ready = sem("spread_ready")
        ident16_ready = sem("ident16_ready")
        bn_var = sem("bn_var")
        bn_rstd = sem("bn_rstd")
        bn_step = sem("bn_step")
        diag_ready = sem("diag_ready")
        s_wide_done = sem("s_wide_done")
        t_col_done = sem("t_col_done")
        t_col_ready = sem("t_col_ready")
        t2_diag_ready = sem("t2_diag_ready")
        c_done = sem("c_done")
        c_ready = sem("c_ready")
        folded = sem("folded")
        abs_ready = sem("abs_ready")
        bound_done = sem("bound_done")
        u_clamped = sem("u_clamped")
        u_ready = sem("u_ready")
        scaled = sem("scaled")
        hi_ready = sem("hi_ready")
        lo_ready = sem("lo_ready")
        u_col_done = sem("u_col_done")
        u_col_ready = sem("u_col_ready")
        iu_col_ready = sem("iu_col_ready")
        bias_ready = sem("bias_ready")
        x_landed = [sem(f"x_landed{i}") for i in range(2)]
        adj_landed = [sem(f"adj_landed{i}") for i in range(2)]
        y_out_free = [sem(f"y_out_free{i}") for i in range(2)]
        stat_a_done, halves_a_done = sem("stat_a_done"), sem("halves_a_done")
        terms_a_done, ve_a_done = sem("terms_a_done"), sem("ve_a_done")
        rstd_a_done, shift_a_done = sem("rstd_a_done"), sem("shift_a_done")
        stat_b_done, halves_b_done = sem("stat_b_done"), sem("halves_b_done")
        terms_b_done, ve_b_done = sem("terms_b_done"), sem("ve_b_done")
        rstd_b_done, shift_b_done = sem("rstd_b_done"), sem("shift_b_done")
        stat_c_done, halves_c_done = sem("stat_c_done"), sem("halves_c_done")
        terms_c_done, ve_c_done = sem("terms_c_done"), sem("ve_c_done")
        rstd_c_done, shift_c_done = sem("rstd_c_done"), sem("shift_c_done")
        xn_turned, wh_done = sem("xn_turned"), sem("wh_done")
        probs_turned, att_done, mlp1_done = sem("probs_turned"), sem("att_done"), sem("mlp1_done")
        mlp2_done, mlp3_done, z_turned = sem("mlp2_done"), sem("mlp3_done"), sem("z_turned")
        x1n_turned, feat_turned, router_done = sem("x1n_turned"), sem("feat_turned"), sem("router_done")
        rw_turned, route_done, y_bias_done = sem("rw_turned"), sem("route_done"), sem("y_bias_done")
        y_turned = sem("y_turned")
        xn_ready = sem("xn_ready")
        xn_t_ready = sem("xn_t_ready")
        xn_wa_ready = sem("xn_wa_ready")
        logits_ready = sem("logits_ready")
        wh_ready = sem("wh_ready")
        leaky_done = sem("leaky_done")
        weighed = sem("weighed")
        top_done = sem("top_done")
        lowered = sem("lowered")
        exp_done = sem("exp_done")
        total_done = sem("total_done")
        inv_total_done = sem("inv_total_done")
        probs_ready = sem("probs_ready")
        probs_t_ready = sem("probs_t_ready")
        att_ready = sem("att_ready")
        mlp1_linear = sem("mlp1_linear")
        mlp1_ready = sem("mlp1_ready")
        mlp2_linear = sem("mlp2_linear")
        mlp2_ready = sem("mlp2_ready")
        z_t_ready = sem("z_t_ready")
        z_ready = sem("z_ready")
        z_normed = sem("z_normed")
        z_gained = sem("z_gained")
        xb_ready = sem("xb_ready")
        x1_ready = sem("x1_ready")
        x1_kept_ready = sem("x1_kept_ready")
        x1n_ready = sem("x1n_ready")
        sum4_done, sum2_done, feat_done = sem("sum4_done"), sem("sum2_done"), sem("feat_done")
        x_hi_ready = sem("x_hi_ready")
        x_lo_ready = sem("x_lo_ready")
        feat_t_ready = sem("feat_t_ready")
        logit_ready = sem("logit_ready")
        neg_top_done = sem("neg_top_done")
        ex_done = sem("ex_done")
        ex_inv_done = sem("ex_inv_done")
        rw_ready = sem("rw_ready")
        rw_hi_ready = sem("rw_hi_ready")
        rw16_ready = sem("rw16_ready")
        rw_t_ready = sem("rw_t_ready")
        rw16_t_ready = sem("rw16_t_ready")
        route_ready = sem("route_ready")
        y_bias_ready = sem("y_bias_ready")
        z1_done = sem("z1_done")
        r1_ready = sem("r1_ready")
        h1_hi_ready = sem("h1_hi_ready")
        h1_lo_ready = sem("h1_lo_ready")
        z2_done = sem("z2_done")
        r2_ready = sem("r2_ready")
        h2_hi_ready = sem("h2_hi_ready")
        h2_lo_ready = sem("h2_lo_ready")
        y_done = sem("y_done")
        y_t_ready = sem("y_t_ready")
        y_out_ready = sem("y_out_ready")

        GNN_LOADS = [(w_sb[:, :], W), (a_col[:, :], a), (w1_sb[:, :], W1), (w2_sb[:, :], W2), (w3_sb[:, :], W3),
                     (b1_col[:, :], b1.rearrange("(p o) -> p o", o=1)),
                     (b2_col[:, :], b2.rearrange("(p o) -> p o", o=1)),
                     (b3_col[:, :], b3.rearrange("(p o) -> p o", o=1)),
                     (lng[:, :], ln_g.partition_broadcast(P)), (lnb[:, :], ln_b.partition_broadcast(P)),
                     (wr_sb[:, :], Wr), (br_sb[:, :], br.partition_broadcast(P))]
        FFN_LOADS = [(bn_g[:, 0, :], g1), (bn_g[:, 1, :], g2), (bn_v[:, 0, :], v1), (bn_v[:, 1, :], v2),
                     (bn_m[:, 0, :], m1), (bn_m[:, 1, :], m2), (bn_b[:, 0, :], be1), (bn_b[:, 1, :], be2),
                     (bn_c[:, 0, :], c1), (bn_c[:, 1, :], c2), (bo_row[:, :], bo),
                     (e1_sb[:, :, :], E1.rearrange("e d h -> d e h")),
                     (e2_sb[:, :, :], E2.rearrange("e d h -> d e h")),
                     (eo_sb[:, :, :], Eo.rearrange("e d h -> d e h"))]

        def wait(eng, s, count):
            if not (isinstance(count, int) and count <= 0):
                eng.wait_ge(s, count)

        def pipeline(eng, body, prepare):
            for n in range(-3, 1):
                body(0, n)
                if n == -3:
                    prepare()
            with eng.Fori(0, (T - 4) // 2) as u:
                body(u, 1)
                body(u, 2)
            for n in range(T - 3, T + 1):
                body(0, n)

        def parts(u, c):
            n = 2 * u + c
            if not isinstance(n, int):
                return n, True, True, True, True, True
            return (n, *(0 <= n + k < T for k in (0, 1, 2, 3, -1)))

        def flat(t):
            return t[:, :, :].rearrange("p b d -> p (b d)")

        block = ctx.enter_context(nc.Block())

        @block.sync
        def _(sp):
            def load(u, c):
                t = 2 * u + c
                wait(sp, xn_ready, t - 1)
                wait(sp, xb_ready, t - 1)
                sp.dma_start(x_in[c % 2][:, :, :], x_t[t]).then_inc(x_landed[c % 2], 16)
                wait(sp, weighed, t - 1)
                for k in range(2):
                    sp.dma_start(adj_in[c % 2][k * C:(k + 1) * C, :, :],
                                 adj_t[t, k, t, k]).then_inc(adj_landed[c % 2], 16)

            for i in range(2):
                sp.sem_inc(y_out_free[i], 16)
            load(0, 0)
            for dst, src in GNN_LOADS:
                sp.dma_start(dst, src).then_inc(gnn_landed, 16)

            def body(u, c):
                n, ffn, has_c, has_b, has_a, last = parts(u, c)
                if has_a and not (isinstance(n, int) and n == -3):
                    load(u, c + 3)
                if last:
                    sp.wait_ge(y_out_ready, n)
                    sp.dma_start(out_t[n - 1], y_out[(c - 1) % 2][:, :, :]).then_inc(y_out_free[(c - 1) % 2], 16)

            def prepare():
                for dst, src in FFN_LOADS:
                    sp.dma_start(dst, src).then_inc(ffn_landed, 16)

            pipeline(sp, body, prepare)
            for i in range(2):
                sp.wait_ge(y_out_free[i], 16 * (T // 2 + 1))

        @block.tensor
        def _(pe):
            def products(dst, hi, lo, m_hi, m_lo, first, last, lo_ready=None):
                for k, (w, m) in enumerate(((hi, m_hi), (lo, m_hi), (hi, m_lo))):
                    if k == 2 and lo_ready is not None:
                        pe.wait_ge(*lo_ready)
                    for j in range(2):
                        cols = slice(j * HALF, (j + 1) * HALF)
                        mm = pe.matmul(dst[:, cols], w, m[:, cols], start=(first and k == 0), stop=(last and k == 2))
                return mm

            def turn(src):
                for b in range(NB):
                    mm = pe.transpose(F[:, b * P:(b + 1) * P], src[:, b * P:(b + 1) * P], ident[:, :])
                return mm

            def wide(w, src):
                for j in range(2):
                    cols = slice(j * HALF, (j + 1) * HALF)
                    mm = pe.matmul(F[:, cols], w, src[:, cols], start=True, stop=True)
                return mm

            pe.wait_ge(ident_ready, 1)
            pe.wait_ge(gnn_landed, 16 * len(GNN_LOADS))
            pe.transpose(F[:, 0:P], w_sb[:, :], ident[:, :]).then_inc(wt_done, 1)
            pe.wait_ge(wt_ready, 1)
            pe.wait_ge(a_wide_ready, 1)
            pe.matmul(F[:, HALF:HALF + P], a_wide[:, :], wt_sb[:, :], start=True, stop=True).then_inc(wa_done, 1)

            def prepare():
                pe.wait_ge(diag_ready, 1)
                pe.wait_ge(consts_ready, 1)
                for layer, dst in ((0, Z1), (1, Z2)):
                    for j in range(2):
                        mm = pe.matmul(dst[:, j * HALF:(j + 1) * HALF], ones[0:NE, :],
                                       s_diag[:, layer, 4 * j:4 * j + 4, :], start=True, stop=True)
                    mm.then_inc(s_wide_done, 1)
                pe.transpose(Y[:, 0:NE], bn_t[:, 0, :], ident[0:NE, 0:NE])
                pe.transpose(Y[:, NE:2 * NE], bn_t[:, 1, :], ident[0:NE, 0:NE]).then_inc(t_col_done, 1)
                pe.wait_ge(t2_diag_ready, 1)
                pe.wait_ge(ffn_landed, 16 * len(FFN_LOADS))
                for e in range(NE):
                    mm = pe.matmul(Y[0:NE, HALF:HALF + P], t2_diag[:, e, :], eo_sb[:, e, :],
                                   start=(e == 0), stop=(e == NE - 1))
                mm.then_inc(c_done, 1)
                for layer, Z, bw, bt in ((0, Z1, bound_x, inv_k1), (1, Z2, bound_h, inv_k2)):
                    pe.wait_ge(abs_ready, layer + 1)
                    pe.wait_ge(diag_ready, 2)
                    for j in range(2):
                        pe.matmul(Z[:, j * HALF:(j + 1) * HALF], bw[:, :], abs_w[:, 4 * j:4 * j + 4, :],
                                  start=True, stop=False)
                        mm = pe.matmul(Z[:, j * HALF:(j + 1) * HALF], bt[:, :],
                                       t_diag[:, layer, 4 * j:4 * j + 4, :], start=False, stop=True)
                    mm.then_inc(bound_done, 1)
                    pe.wait_ge(u_ready, layer + 1)
                    for e in range(NE):
                        mm = pe.matmul(Z[:, e:e + 1], u_wide[:, e, :], ident[:, 0:1], start=True, stop=True)
                    mm.then_inc(u_col_done, 1)
                pe.wait_ge(abs_ready, 3)
                pe.wait_ge(u_col_ready, 1)
                for e in range(NE):
                    mm = pe.matmul(Z1[:, 0:P], bound_o[:, :], abs_w[:, e, :], start=(e == 0), stop=(e == NE - 1))
                mm.then_inc(bound_done, 1)
                pe.wait_ge(u_ready, 3)
                pe.matmul(Z1[:, 0:1], uo_wide[:, :], ident[:, 0:1], start=True, stop=True).then_inc(u_col_done, 1)

            read_out = [(wa_ready, 1)]

            def body(u, c):
                n, ffn, has_c, has_b, has_a, last = parts(u, c)
                if not isinstance(n, int) or n == T - 3:
                    read_out[0] = (route_ready, n + 1)

                def claim(then, count):
                    pe.wait_ge(*read_out[0])
                    read_out[0] = (then, count)

                def front(gap):
                    m = n + 2
                    if gap == 0 and has_b:
                        claim(probs_t_ready, m + 1)
                        pe.wait_ge(probs_ready, m + 1)
                        turn(probs[c % 2][:, :, :, :].rearrange("p b k j -> p (b k j)")).then_inc(probs_turned, 1)
                    if gap == 3 and has_b:
                        claim(att_ready, m + 1)
                        pe.wait_ge(probs_t_ready, m + 1)
                        pe.wait_ge(wh_ready, m + 1)
                        for b in range(NB):
                            mm = pe.matmul(F[:, b * P:(b + 1) * P], wh[c % 2][:, b, :], probs_t[:, b, :],
                                           start=True, stop=True)
                        mm.then_inc(att_done, 1)
                    if gap == 5 and has_b:
                        claim(mlp1_linear, m + 1)
                        pe.wait_ge(att_ready, m + 1)
                        wide(w1_sb[:, :], att).then_inc(mlp1_done, 1)
                    if gap == 10 and has_b:
                        claim(mlp2_linear, m + 1)
                        pe.wait_ge(mlp1_ready, m + 1)
                        wide(w2_sb[:, :], mlp1).then_inc(mlp2_done, 1)
                    if gap == 13 and has_b:
                        claim(z_t_ready, m + 1)
                        pe.wait_ge(mlp2_ready, m + 1)
                        wide(w3_sb[:, :], mlp2).then_inc(mlp3_done, 1)
                    if gap == 16 and has_b:
                        claim(z_ready, m + 1)
                        pe.wait_ge(z_t_ready, m + 1)
                        turn(z_t).then_inc(z_turned, 1)
                    m = n + 3
                    if gap == 12 and has_a:
                        claim(xn_t_ready, m + 1)
                        pe.wait_ge(xn_ready, m + 1)
                        turn(flat(xn)).then_inc(xn_turned, 1)
                    if gap == 19 and has_a:
                        claim(wh_ready, m + 1)
                        pe.wait_ge(xn_t_ready, m + 1)
                        for b in range(NB):
                            mm = pe.matmul(F[:, b * P:(b + 1) * P], xn_t[:, b * P:(b + 1) * P], w_sb[:, :],
                                           start=True, stop=True)
                        mm.then_inc(wh_done, 1)
                    m = n + 1
                    if gap == 8 and has_c:
                        claim(x_lo_ready, m + 1)
                        pe.wait_ge(x1n_ready, m + 1)
                        turn(flat(x1n)).then_inc(x1n_turned, 1)
                    if gap == 15 and has_c:
                        claim(feat_t_ready, m + 1)
                        pe.wait_ge(feat_done, m + 1)
                        pe.transpose(F[:, 0:P], feat[:, :], ident[:, :]).then_inc(feat_turned, 1)
                    if gap == 17 and has_c:
                        claim(logit_ready, m + 1)
                        pe.wait_ge(feat_t_ready, m + 1)
                        pe.matmul(F[:, 0:NE], feat_t[:, :], wr_sb[:, :], start=True, stop=True).then_inc(router_done, 1)
                    if gap == 21 and has_c:
                        claim(rw16_t_ready, m + 1)
                        pe.wait_ge(rw16_ready, m + 1)
                        if isinstance(n, int) and n == -1:
                            pe.wait_ge(ident16_ready, 1)
                        pe.transpose(F[0:NE, 0:P], rw[:, :], ident[:, :])
                        pe.transpose(F[0:2 * NE, HALF:HALF + P // 2].bitcast(F16), rw16[:, :],
                                     ident16[:, :]).then_inc(rw_turned, 1)
                    if gap == 22 and has_c:
                        claim(route_ready, m + 1)
                        if isinstance(n, int) and n == -1:
                            pe.wait_ge(spread_ready, 1)
                        for e in range(NE):
                            mm = pe.matmul(F[:, e * P:(e + 1) * P], spread[:, e, :], rw16_t[:, :],
                                           start=True, stop=True)
                        mm.then_inc(route_done, 1)
                    if gap == 14 and ffn:
                        claim(y_bias_ready, n + 1)
                        if isinstance(n, int) and n == 0:
                            pe.wait_ge(c_ready, 1)
                        pe.wait_ge(rw_t_ready, n + 1)
                        pe.matmul(F[:, 0:P], c_row[:, :], rw_t[:, :], start=True, stop=True).then_inc(y_bias_done, 1)
                    if gap == 6 and last:
                        claim(y_out_ready, n)
                        pe.wait_ge(y_t_ready, n)
                        turn(y_t).then_inc(y_turned, 1)

                for e in range(NE):
                    g = NE * n + e
                    if ffn:
                        if isinstance(n, int) and n == 0 and e == 0:
                            pe.wait_ge(lo_ready, 3)
                        if e == 0:
                            pe.wait_ge(x_hi_ready, n + 1)
                        wait(pe, r1_ready, g)
                        products(Z1, e1_hi[:, e, :], e1_lo[:, e, :], x_hi[c % 2], x_lo[c % 2], True, True,
                                 (x_lo_ready, n + 1) if e == 0 else None).then_inc(z1_done, 1)
                    front(3 * e)
                    if (ffn and not (isinstance(g, int) and g == 0)) or (not ffn and last and e == 0):
                        k = (e - 1) % NE
                        wait(pe, h2_lo_ready, g - 1)
                        pe.wait_ge(h1_hi_ready, g)
                        products(Z2, e2_hi[:, k, :], e2_lo[:, k, :], h1_hi[k % 2], h1_lo[k % 2],
                                 True, True, (h1_lo_ready, g)).then_inc(z2_done, 1)
                    front(3 * e + 1)
                    if (ffn and not (isinstance(g, int) and g <= 1)) or (not ffn and last and e <= 1):
                        k = (e - 2) % NE
                        pe.wait_ge(h2_hi_ready, g - 1)
                        if k == 0:
                            wait(pe, y_t_ready, n)
                        products(Y, eo_hi[:, k, :], eo_lo[:, k, :], h2_hi[k % 2], h2_lo[k % 2], k == 0, k == NE - 1,
                                 (h2_lo_ready, g - 1)).then_inc(y_done, 1)
                    front(3 * e + 2)

            pipeline(pe, body, prepare)

        @block.scalar
        def _(act):
            def prepare():
                for layer, w, hi in ((0, e1_sb, e1_hi), (1, e2_sb, e2_hi), (2, eo_sb, eo_hi)):
                    act.wait_ge(folded, (1, 3, 4)[layer])
                    if layer > 0:
                        act.wait_ge(bound_done, layer)
                    act.activation(abs_w[:, :, :], w[:, :, :], ACT.Abs).then_inc(abs_ready, 1)
                    act.wait_ge(scaled, layer + 1)
                    act.activation(hi[:, :, :], w[:, :, :], ACT.Copy).then_inc(hi_ready, 1)

            def body(u, c):
                n, ffn, has_c, has_b, has_a, last = parts(u, c)

                def front(e, place):
                    at = (e, place)
                    m = n + 2
                    if at == (0, 0) and has_b:
                        act.wait_ge(probs_turned, m + 1)
                        wait(act, att_done, m)
                        act.activation(flat(probs_t), F[:, :], ACT.Copy).then_inc(probs_t_ready, 1)
                    if at == (1, 0) and has_b:
                        act.wait_ge(att_done, m + 1)
                        wait(act, z_t_ready, m)
                        act.activation(att[:, :], F[:, :], ACT.Copy).then_inc(att_ready, 1)
                    if at == (1, 2) and has_b:
                        act.wait_ge(mlp1_done, m + 1)
                        wait(act, mlp2_done, m)
                        act.activation(mlp1[:, :], F[:, :], ACT.Identity, bias=b1_col[:, 0:1]).then_inc(mlp1_linear, 1)
                    if at == (3, 1) and has_b:
                        act.wait_ge(mlp2_done, m + 1)
                        wait(act, mlp3_done, m)
                        act.activation(mlp2[:, :], F[:, :], ACT.Identity, bias=b2_col[:, 0:1]).then_inc(mlp2_linear, 1)
                    if at == (5, 1) and has_b:
                        act.wait_ge(z_turned, m + 1)
                        wait(act, x1_ready, m)
                        act.activation(flat(z), F[:, :], ACT.Copy).then_inc(z_ready, 1)
                    pieces = {(7, 1): (0, 3), (7, 2): (3, NB)}.get(at)
                    if pieces and has_b:
                        if pieces[0] == 0:
                            act.wait_ge(shift_b_done, m + 1)
                        for b in range(*pieces):
                            i = act.activation(z[:, b, :], z[:, b, :], ACT.Identity,
                                               bias=shift_b[:, b:b + 1], scale=rstd_b[:, b:b + 1])
                        if pieces[1] == NB:
                            i.then_inc(z_normed, 1)
                    m = n + 3
                    pieces = {(1, 1): (0, 2), (2, 0): (2, 4), (2, 1): (4, 6), (3, 0): (6, NB)}.get(at)
                    if pieces and has_a:
                        if pieces[0] == 0:
                            act.wait_ge(shift_a_done, m + 1)
                            wait(act, xn_turned, m)
                            wait(act, xn_wa_ready, m)
                        for b in range(*pieces):
                            i = act.activation(xn[:, b, :], x_in[(c + 3) % 2][:, b, :], ACT.Identity,
                                               bias=shift_a[:, b:b + 1], scale=rstd_a[:, b:b + 1])
                        if pieces[1] == NB:
                            i.then_inc(xn_ready, 1)
                    if at == (4, 0) and has_a:
                        act.wait_ge(xn_turned, m + 1)
                        wait(act, wh_done, m)
                        act.activation(xn_t[:, :], F[:, :], ACT.Copy).then_inc(xn_t_ready, 1)
                    if at == (6, 2) and has_a:
                        act.wait_ge(lowered, m + 1)
                        act.activation(scores[:, :, :], scores[:, :, :], ACT.Exp).then_inc(exp_done, 1)
                    if at == (6, 1) and has_a:
                        act.wait_ge(wh_done, m + 1)
                        wait(act, att_done, m - 1)
                        act.activation(flat(wh[(c + 3) % 2]), F[:, :], ACT.Copy).then_inc(wh_ready, 1)
                    m = n + 1
                    if at == (2, 2) and has_c:
                        act.wait_ge(x1n_turned, m + 1)
                        wait(act, z1_done, NE * (m - 1))
                        act.activation(x_hi[(c + 1) % 2][:, :], F[:, :], ACT.Copy).then_inc(x_hi_ready, 1)
                    if at == (5, 0) and has_c:
                        act.wait_ge(feat_turned, m + 1)
                        wait(act, router_done, m)
                        act.activation(feat_t[:, :], F[:, 0:P], ACT.Copy, scale=1.0 / NB).then_inc(feat_t_ready, 1)
                    if at == (6, 0) and has_c:
                        act.wait_ge(neg_top_done, m + 1)
                        act.activation(ex[:, :], logit[:, :], ACT.Exp, bias=neg_top[:, 0:1],
                                       accum_out=ex_sum[:, 0:1]).then_inc(ex_done, 1)
                    if at == (7, 0) and has_c:
                        act.wait_ge(rw_turned, m + 1)
                        wait(act, y_bias_done, m)
                        act.activation(rw_t[:, :], F[0:NE, 0:P], ACT.Copy).then_inc(rw_t_ready, 1)
                        act.activation(rw16_t[:, :], F[0:2 * NE, HALF:HALF + P // 2].bitcast(F16),
                                       ACT.Copy).then_inc(rw16_t_ready, 1)
                    if at == (7, 1) and has_c:
                        act.wait_ge(route_done, m + 1)
                        wait(act, r2_ready, NE * (m - 1))
                        act.activation(flat(route[(c + 1) % 2]), F[:, :], ACT.Copy).then_inc(route_ready, 1)
                    if at == (4, 2) and ffn:
                        act.wait_ge(y_bias_done, n + 1)
                        wait(act, y_t_ready, n)
                        act.activation(y_bias[:, :], F[:, 0:P], ACT.Copy).then_inc(y_bias_ready, 1)

                for e in range(NE):
                    g = NE * n + e
                    i = e % 2
                    if ffn:
                        if isinstance(n, int) and n == 0 and e == 0:
                            act.wait_ge(bias_ready, 1)
                        act.wait_ge(z1_done, g + 1)
                        wait(act, h1_lo_ready, g - 1)
                        act.activation(r1[i][:, :], Z1[:, :], ACT.Relu, bias=bias1[:, e:e + 1]).then_inc(r1_ready, 1)
                    front(e, 0)
                    if ffn:
                        act.wait_ge(r1_ready, g + 1)
                        wait(act, z2_done, g - 1)
                        act.activation(h1_hi[i][:, :], r1[i][:, :], ACT.Copy).then_inc(h1_hi_ready, 1)
                    front(e, 1)
                    if (ffn and not (isinstance(g, int) and g == 0)) or (not ffn and last and e == 0):
                        act.wait_ge(r2_ready, g)
                        wait(act, y_done, g - 2)
                        act.activation(h2_hi[1 - i][:, :], Z2[:, :], ACT.Copy).then_inc(h2_hi_ready, 1)
                    front(e, 2)

            pipeline(act, body, prepare)

        @block.vector
        def _(dve):
            def norm_stats(src, tiles, sems, m):
                stat, mean2, gap, ve = tiles
                stat_done, halves_done, terms_done, ve_done = sems
                for b in range(NB):
                    i = dve.bn_stats(stat[:, b, :], src[:, b, :])
                i.then_inc(stat_done, 1)
                dve.wait_ge(stat_done, m + 1)
                dve.tensor_tensor(gap[:, :], stat[:, :, 1], stat[:, :, 4], ALU.subtract)
                dve.tensor_tensor(ve[:, :], stat[:, :, 2], stat[:, :, 5], ALU.add)
                dve.tensor_tensor(mean2[:, :], stat[:, :, 1], stat[:, :, 4], ALU.add).then_inc(halves_done, 1)
                dve.wait_ge(halves_done, m + 1)
                dve.scalar_tensor_tensor(gap[:, :], gap[:, :], 0.25, gap[:, :], ALU.mult, ALU.mult)
                dve.tensor_scalar(ve[:, :], ve[:, :], 1.0 / D, LN_EPS, ALU.mult, ALU.add).then_inc(terms_done, 1)
                dve.wait_ge(terms_done, m + 1)
                dve.tensor_tensor(ve[:, :], ve[:, :], gap[:, :], ALU.add).then_inc(ve_done, 1)

            def norm_shift(shift, mean2, rstd, rstd_done, shift_done, m):
                dve.wait_ge(rstd_done, m + 1)
                dve.scalar_tensor_tensor(shift[:, :], mean2[:, :], -0.5, rstd[:, :], ALU.mult,
                                         ALU.mult).then_inc(shift_done, 1)

            def leaky(h, linear, ready, m):
                dve.wait_ge(linear, m + 1)
                dve.scalar_tensor_tensor(h[:, :], h[:, :], MLP_ALPHA, h[:, :], ALU.mult, ALU.max).then_inc(ready, 1)

            def over_heads(col, like):
                return col[:, :].unsqueeze(2).broadcast_to([P, NB, like])

            dve.wait_ge(consts_ready, 1)
            dve.wait_ge(gnn_landed, 16 * len(GNN_LOADS))
            dve.tensor_scalar(a_wide[:, :], ones[:, :], a_col[:, 0:1], None, ALU.mult).then_inc(a_wide_ready, 1)
            dve.wait_ge(wt_done, 1)
            dve.tensor_copy(wt_sb[:, :], F[:, 0:P]).then_inc(wt_ready, 1)
            dve.wait_ge(wa_done, 1)
            dve.tensor_copy(wa_wide[:, :], F[:, HALF:HALF + P]).then_inc(wa_ready, 1)
            dve.wait_ge(ident_ready, 1)
            dve.tensor_tensor(pick[:, :], ident[0:2 * NE, 0:NE], ident[0:2 * NE, NE:2 * NE],
                              ALU.add).then_inc(pick_ready, 1)
            dve.wait_ge(pick_ready, 1)
            dve.tensor_copy(spread[:, :, :], pick[:, :].unsqueeze(2).broadcast_to([2 * NE, NE, P])
                            ).then_inc(spread_ready, 1)
            dve.tensor_copy(ident16[:, :], ident[:, :]).then_inc(ident16_ready, 1)

            def prepare():
                dve.wait_ge(ffn_landed, 16 * len(FFN_LOADS))
                dve.tensor_scalar(bn_v[:, :, :], bn_v[:, :, :], BN_EPS, None, ALU.add).then_inc(bn_var, 1)
                dve.tensor_tensor(bn_t[:, :, :], bn_c[:, :, :], bn_m[:, :, :], ALU.subtract).then_inc(bn_step, 1)
                dve.wait_ge(bn_rstd, 1)
                dve.tensor_tensor(bn_s[:, :, :], bn_g[:, :, :], bn_v[:, :, :], ALU.mult).then_inc(bn_step, 1)
                dve.wait_ge(bn_step, 2)
                dve.tensor_tensor(bn_t[:, :, :], bn_t[:, :, :], bn_s[:, :, :], ALU.mult).then_inc(bn_step, 1)
                dve.wait_ge(bn_step, 3)
                dve.tensor_tensor(bn_t[:, :, :], bn_t[:, :, :], bn_b[:, :, :], ALU.add).then_inc(bn_step, 1)
                dve.wait_ge(bn_step, 4)
                dve.scalar_tensor_tensor(bn_abs[:, :, :], bn_t[:, :, :], -1.0, bn_t[:, :, :], ALU.mult,
                                         ALU.max).then_inc(bn_step, 1)
                dve.wait_ge(bn_step, 5)
                mask = ident[0:NE, 0:NE].unsqueeze(2).broadcast_to([NE, NE, P])
                for src, dst in ((bn_s, s_diag), (bn_abs, t_diag)):
                    for layer in range(2):
                        i = dve.tensor_tensor(dst[:, layer, :, :], mask,
                                              src[:, layer, :].unsqueeze(1).broadcast_to([NE, NE, P]), ALU.mult)
                    i.then_inc(diag_ready, 1)
                dve.wait_ge(s_wide_done, 1)
                dve.tensor_tensor(flat(e1_sb), flat(e1_sb), Z1[:, :], ALU.mult).then_inc(folded, 1)
                dve.wait_ge(s_wide_done, 2)
                dve.tensor_tensor(flat(e2_sb), flat(e2_sb), Z2[:, :], ALU.mult).then_inc(folded, 1)
                dve.wait_ge(t_col_done, 1)
                dve.tensor_copy(t_col[:, :, :].rearrange("p l e -> p (l e)"), Y[:, 0:2 * NE]).then_inc(t_col_ready, 1)
                dve.wait_ge(t_col_ready, 1)
                dve.wait_ge(same_ready, 1)
                dve.tensor_tensor(t2_diag[:, :, :], same_e[:, :].rearrange("p (e f) -> p e f", f=NE),
                                  t_col[:, 1, :].unsqueeze(2).broadcast_to([P, NE, NE]), ALU.mult).then_inc(t2_diag_ready, 1)
                dve.wait_ge(c_done, 1)
                dve.tensor_tensor(c_row[:, :], Y[0:NE, HALF:HALF + P], bo_row[:, :], ALU.add).then_inc(c_ready, 1)

                for layer, Z, w, hi, lo in ((0, Z1, e1_sb, e1_hi, e1_lo), (1, Z2, e2_sb, e2_hi, e2_lo)):
                    if layer == 1:
                        dve.wait_ge(iu_col_ready, 1)
                        dve.tensor_tensor(w[:, :, :], w[:, :, :], iu_col[:, 0, :].unsqueeze(2).broadcast_to([P, NE, P]),
                                          ALU.mult).then_inc(folded, 1)
                    dve.wait_ge(bound_done, layer + 1)
                    dve.tensor_scalar(flat(u_wide), Z[:, :], 1e-30, None, ALU.max).then_inc(u_clamped, 1)
                    dve.wait_ge(u_clamped, layer + 1)
                    dve.reciprocal(flat(u_wide), flat(u_wide)).then_inc(u_ready, 1)
                    dve.wait_ge(u_ready, layer + 1)
                    dve.tensor_tensor(flat(w), flat(w), flat(u_wide), ALU.mult).then_inc(scaled, 1)
                    dve.wait_ge(hi_ready, layer + 1)
                    dve.tensor_tensor(flat(lo), flat(w), flat(hi), ALU.subtract).then_inc(lo_ready, 1)
                    dve.wait_ge(u_col_done, layer + 1)
                    dve.tensor_copy(u_col[:, layer, :], Z[:, 0:NE]).then_inc(u_col_ready, 1)
                    dve.wait_ge(u_col_ready, layer + 1)
                    dve.reciprocal(iu_col[:, layer, :], u_col[:, layer, :]).then_inc(iu_col_ready, 1)
                dve.tensor_tensor(bias1[:, :], t_col[:, 0, :], u_col[:, 0, :], ALU.mult)
                dve.scalar_tensor_tensor(neg_bias2[:, :], t_col[:, 1, :], -1.0, u_col[:, 1, :], ALU.mult,
                                         ALU.mult).then_inc(bias_ready, 1)
                dve.wait_ge(iu_col_ready, 2)
                dve.tensor_tensor(eo_sb[:, :, :], eo_sb[:, :, :], iu_col[:, 1, :].unsqueeze(2).broadcast_to([P, NE, P]),
                                  ALU.mult).then_inc(folded, 1)
                dve.wait_ge(bound_done, 3)
                dve.tensor_scalar(uo_wide[:, :], Z1[:, 0:P], 1e-30, None, ALU.max).then_inc(u_clamped, 1)
                dve.wait_ge(u_clamped, 3)
                dve.reciprocal(uo_wide[:, :], uo_wide[:, :]).then_inc(u_ready, 1)
                dve.wait_ge(u_ready, 3)
                dve.tensor_tensor(eo_sb[:, :, :], eo_sb[:, :, :], uo_wide[:, :].unsqueeze(1).broadcast_to([P, NE, P]),
                                  ALU.mult).then_inc(scaled, 1)
                dve.wait_ge(hi_ready, 3)
                dve.tensor_tensor(flat(eo_lo), flat(eo_sb), flat(eo_hi), ALU.subtract).then_inc(lo_ready, 1)
                dve.wait_ge(u_col_done, 3)
                dve.reciprocal(iuo_col[:, :], Z1[:, 0:1]).then_inc(iu_col_ready, 1)

            def body(u, c):
                n, ffn, has_c, has_b, has_a, last = parts(u, c)

                def front(e, place):
                    at = (e, place)
                    m = n + 1
                    if at == (0, 1) and has_c:
                        dve.wait_ge(z_normed, m + 1)
                        dve.tensor_tensor(z[:, :, :], z[:, :, :], lng[:, :].unsqueeze(1).broadcast_to([P, NB, P]),
                                          ALU.mult).then_inc(z_gained, 1)
                        dve.wait_ge(z_gained, m + 1)
                        dve.wait_ge(xb_ready, m + 1)
                        wait(dve, x1_kept_ready, m - 1)
                        dve.tensor_tensor(x1[(c + 1) % 2][:, :, :], z[:, :, :], xb[:, :, :], ALU.add).then_inc(x1_ready, 1)
                    if at == (0, 2) and has_c:
                        dve.wait_ge(x1_ready, m + 1)
                        norm_stats(x1[(c + 1) % 2], (stat_c, mean2_c, gap_c, ve_c),
                                   (stat_c_done, halves_c_done, terms_c_done, ve_c_done), m)
                    if at == (1, 2) and has_c:
                        norm_shift(shift_c, mean2_c, rstd_c, rstd_c_done, shift_c_done, m)
                        dve.wait_ge(shift_c_done, m + 1)
                        wait(dve, x1n_turned, m)
                        wait(dve, sum4_done, m)
                        for b in range(NB):
                            i = dve.tensor_scalar(x1n[:, b, :], x1[(c + 1) % 2][:, b, :], rstd_c[:, b:b + 1],
                                                  shift_c[:, b:b + 1], ALU.mult, ALU.add)
                        i.then_inc(x1n_ready, 1)
                    if at == (2, 2) and has_c:
                        dve.wait_ge(x_hi_ready, m + 1)
                        dve.tensor_tensor(x_lo[(c + 1) % 2][:, :], F[:, :], x_hi[(c + 1) % 2][:, :],
                                          ALU.subtract).then_inc(x_lo_ready, 1)
                    if at == (5, 2) and has_c:
                        dve.wait_ge(router_done, m + 1)
                        dve.tensor_tensor(logit[:, :], F[:, 0:NE], br_sb[:, :], ALU.add).then_inc(logit_ready, 1)
                        dve.wait_ge(logit_ready, m + 1)
                        dve.tensor_reduce(neg_top[:, :], logit[:, :], AX, ALU.max, negate=True
                                          ).then_inc(neg_top_done, 1)
                    if at == (6, 1) and has_c:
                        dve.wait_ge(ex_done, m + 1)
                        dve.reciprocal(ex_inv[:, :], ex_sum[:, :]).then_inc(ex_inv_done, 1)
                        dve.wait_ge(ex_inv_done, m + 1)
                        wait(dve, rw_turned, m)
                        dve.tensor_scalar(rw[:, :], ex[:, :], ex_inv[:, 0:1], None, ALU.mult).then_inc(rw_ready, 1)
                        dve.wait_ge(rw_ready, m + 1)
                        dve.tensor_copy(rw16[:, 0:NE], rw[:, :]).then_inc(rw_hi_ready, 1)
                        dve.wait_ge(rw_hi_ready, m + 1)
                        dve.tensor_tensor(rw16[:, NE:2 * NE], rw[:, :], rw16[:, 0:NE],
                                          ALU.subtract).then_inc(rw16_ready, 1)
                    m = n + 3
                    if at == (0, 0) and has_a:
                        dve.wait_ge(x_landed[(c + 3) % 2], 16 * (u + (c + 3) // 2 + 1))
                        norm_stats(x_in[(c + 3) % 2], (stat_a, mean2_a, gap_a, ve_a),
                                   (stat_a_done, halves_a_done, terms_a_done, ve_a_done), m)
                    if at == (1, 0) and has_a:
                        wait(dve, xn_ready, m)
                        norm_shift(shift_a, mean2_a, rstd_a, rstd_a_done, shift_a_done, m)
                    if at == (4, 2) and has_a:
                        dve.wait_ge(xn_wa_ready, m + 1)
                        dve.tensor_reduce(factor[:, :], xn_wa[:, :, :], AX, ALU.add).then_inc(logits_ready, 1)
                        dve.wait_ge(logits_ready, m + 1)
                        dve.scalar_tensor_tensor(factor[:, :], factor[:, :], ALPHA, factor[:, :], ALU.mult,
                                                 ALU.max).then_inc(leaky_done, 1)
                    if at == (5, 1) and has_a:
                        dve.wait_ge(leaky_done, m + 1)
                        dve.wait_ge(adj_landed[(c + 3) % 2], 32 * (u + (c + 3) // 2 + 1))
                        dve.tensor_tensor(scores[:, :, :], adj_in[(c + 3) % 2][:, :, :], over_heads(factor, C),
                                          ALU.mult).then_inc(weighed, 1)
                        dve.wait_ge(weighed, m + 1)
                        dve.tensor_reduce(top[:, :], scores[:, :, :], AX, ALU.max).then_inc(top_done, 1)
                    if at == (6, 0) and has_a:
                        dve.wait_ge(top_done, m + 1)
                        dve.tensor_tensor(scores[:, :, :], scores[:, :, :], over_heads(top, C),
                                          ALU.subtract).then_inc(lowered, 1)
                    if at == (7, 0) and has_a:
                        dve.wait_ge(exp_done, m + 1)
                        dve.tensor_reduce(total[:, :], scores[:, :, :], AX, ALU.add).then_inc(total_done, 1)
                        dve.wait_ge(total_done, m + 1)
                        dve.reciprocal(inv_total[:, :], total[:, :]).then_inc(inv_total_done, 1)
                    if at == (7, 1) and has_a:
                        dve.wait_ge(inv_total_done, m + 1)
                        wait(dve, probs_turned, m - 1)
                        if isinstance(n, int) and n == -3:
                            dve.wait_ge(probs_zero, 2)
                        for k in range(2):
                            rows = slice(k * C, (k + 1) * C)
                            i = dve.tensor_tensor(probs[(c + 3) % 2][rows, :, k, :], scores[rows, :, :],
                                                  inv_total[rows, :].unsqueeze(2).broadcast_to([C, NB, C]), ALU.mult)
                        i.then_inc(probs_ready, 1)
                    m = n + 2
                    if at == (2, 1) and has_b:
                        leaky(mlp1, mlp1_linear, mlp1_ready, m)
                    if at == (3, 2) and has_b:
                        leaky(mlp2, mlp2_linear, mlp2_ready, m)
                    if at == (4, 1) and has_b:
                        dve.wait_ge(mlp3_done, m + 1)
                        wait(dve, z_turned, m)
                        dve.scalar_tensor_tensor(z_t[:, :], F[:, :], b3_col[:, 0:1], att[:, :], ALU.add,
                                                 ALU.add).then_inc(z_t_ready, 1)
                    if at == (5, 2) and has_b:
                        dve.wait_ge(z_ready, m + 1)
                        norm_stats(z, (stat_b, mean2_b, gap_b, ve_b),
                                   (stat_b_done, halves_b_done, terms_b_done, ve_b_done), m)
                    if at == (6, 2) and has_b:
                        wait(dve, z_normed, m)
                        norm_shift(shift_b, mean2_b, rstd_b, rstd_b_done, shift_b_done, m)
                    if at == (1, 1) and last:
                        dve.wait_ge(y_done, NE * n)
                        dve.wait_ge(y_bias_ready, n)
                        dve.scalar_tensor_tensor(y_t[:, :].rearrange("p (b q) -> p b q", q=P),
                                                 Y[:, :].rearrange("p (b q) -> p b q", q=P), iuo_col[:, 0:1],
                                                 y_bias[:, :].unsqueeze(1).broadcast_to([P, NB, P]),
                                                 ALU.mult, ALU.add).then_inc(y_t_ready, 1)
                    if at == (2, 0) and last:
                        dve.wait_ge(y_turned, n)
                        dve.wait_ge(x1_kept_ready, n)
                        dve.wait_ge(y_out_free[(c - 1) % 2], 16 * (u + (c - 1) // 2 + 1))
                        dve.tensor_tensor(flat(y_out[(c - 1) % 2]), F[:, :], flat(x1_kept[(c - 1) % 2]),
                                          ALU.add).then_inc(y_out_ready, 1)

                for e in range(NE):
                    g = NE * n + e
                    k = (e - 1) % NE
                    step = (ffn and not (isinstance(g, int) and g == 0)) or (not ffn and last and e == 0)
                    front(e, 0)
                    if step:
                        dve.wait_ge(z2_done, g)
                        if isinstance(g, int) and g == 1:
                            dve.wait_ge(bias_ready, 1)
                            dve.wait_ge(iu_col_ready, 3)
                        if k == 0:
                            dve.wait_ge(route_ready, n + 1)
                        Z = Z2[:, :].rearrange("p (b q) -> p b q", q=P)
                        par = (c - 1) % 2 if e == 0 else c % 2
                        dve.scalar_tensor_tensor(Z, Z, neg_bias2[:, k:k + 1],
                                                 route[par][:, k, :].unsqueeze(1).broadcast_to([P, NB, P]),
                                                 ALU.max, ALU.mult).then_inc(r2_ready, 1)
                    front(e, 1)
                    if step:
                        dve.wait_ge(h2_hi_ready, g)
                        wait(dve, y_done, g - 2)
                        dve.tensor_tensor(h2_lo[k % 2][:, :], Z2[:, :], h2_hi[k % 2][:, :],
                                          ALU.subtract).then_inc(h2_lo_ready, 1)
                    front(e, 2)

            pipeline(dve, body, prepare)

        @block.gpsimd
        def _(pool):
            pool.memset(ident[:, :], 0.0).then_inc(ident_zero, 1)
            pool.memset(same_e[:, :], 0.0).then_inc(same_zero, 1)
            pool.wait_ge(ident_zero, 1)
            pool.affine_select(out=ident[:, :], in_=ident[:, :], compare_op=ALU.not_equal, fill=1.0, base=0,
                               pattern=[[-1, P]], channel_multiplier=1).then_inc(ident_ready, 1)
            for t, value in ((ones, 1.0), (bound_x, X_BOUND / K1), (bound_h, K1 / K2), (bound_o, 1.0 / K3),
                             (inv_k1, 1.0 / K1), (inv_k2, 1.0 / K2), (neg_half, -0.5)):
                i = pool.memset(t[:, :], value)
            i.then_inc(consts_ready, 1)
            pool.wait_ge(same_zero, 1)
            pool.memset(same_e[:, 0:NE * NE:NE + 1], 1.0).then_inc(same_ready, 1)
            for t in probs:
                pool.memset(t[:, :, :, :], 0.0).then_inc(probs_zero, 1)
            pool.wait_ge(consts_ready, 1)

            def rstd_of(ve, rstd, ve_done, rstd_done, m):
                pool.wait_ge(ve_done, m + 1)
                pool.tensor_tensor(rstd[:, :], ve[:, :], neg_half[:, 0:NB], ALU.pow).then_inc(rstd_done, 1)

            def prepare():
                pool.wait_ge(bn_var, 1)
                v = bn_v[:, :, :].rearrange("e l h -> e (l h)")
                pool.tensor_tensor(v, v, neg_half[0:NE, :], ALU.pow).then_inc(bn_rstd, 1)

            def body(u, c):
                n, ffn, has_c, has_b, has_a, last = parts(u, c)

                def front(e):
                    m = n + 3
                    if e == 0 and has_a:
                        wait(pool, xn_ready, m)
                        rstd_of(ve_a, rstd_a, ve_a_done, rstd_a_done, m)
                    if e == 4 and has_a:
                        pool.wait_ge(xn_ready, m + 1)
                        wait(pool, logits_ready, m)
                        pool.tensor_tensor(xn_wa[:, :, :], xn[:, :, :],
                                           wa_wide[:, :].unsqueeze(1).broadcast_to([P, NB, P]), ALU.mult
                                           ).then_inc(xn_wa_ready, 1)
                    m = n + 1
                    if e == 1 and has_c:
                        rstd_of(ve_c, rstd_c, ve_c_done, rstd_c_done, m)
                    if e == 2 and has_c:
                        pool.wait_ge(x1n_ready, m + 1)
                        pool.tensor_tensor(sum4[:, :, :], x1n[:, 0:4, :], x1n[:, 4:8, :], ALU.add).then_inc(sum4_done, 1)
                    if e == 3 and has_c:
                        pool.wait_ge(sum4_done, m + 1)
                        pool.tensor_tensor(sum2[:, :, :], sum4[:, 0:2, :], sum4[:, 2:4, :], ALU.add).then_inc(sum2_done, 1)
                        pool.wait_ge(sum2_done, m + 1)
                        wait(pool, feat_turned, m)
                        pool.tensor_tensor(feat[:, :], sum2[:, 0, :], sum2[:, 1, :], ALU.add).then_inc(feat_done, 1)
                    if e == 5 and has_c:
                        wait(pool, y_out_ready, m - 1)
                        pool.wait_ge(x1_ready, m + 1)
                        pool.tensor_tensor(x1_kept[(c + 1) % 2][:, :, :], x1[(c + 1) % 2][:, :, :],
                                           ones[:, :].unsqueeze(1).broadcast_to([P, NB, P]), ALU.mult
                                           ).then_inc(x1_kept_ready, 1)
                    m = n + 2
                    if e == 6 and has_b:
                        pool.wait_ge(x_landed[c % 2], 16 * (u + (c + 2) // 2 + 1))
                        if isinstance(n, int) and n == -2:
                            pool.wait_ge(gnn_landed, 16 * len(GNN_LOADS))
                        wait(pool, x1_ready, m)
                        pool.tensor_tensor(xb[:, :, :], x_in[c % 2][:, :, :],
                                           lnb[:, :].unsqueeze(1).broadcast_to([P, NB, P]), ALU.add
                                           ).then_inc(xb_ready, 1)
                    if e == 7 and has_b:
                        wait(pool, z_normed, m)
                        rstd_of(ve_b, rstd_b, ve_b_done, rstd_b_done, m)

                for e in range(NE):
                    g = NE * n + e
                    if ffn:
                        pool.wait_ge(h1_hi_ready, g + 1)
                        wait(pool, z2_done, g - 1)
                        pool.tensor_tensor(h1_lo[e % 2][:, :], r1[e % 2][:, :], h1_hi[e % 2][:, :],
                                           ALU.subtract).then_inc(h1_lo_ready, 1)
                    front(e)

            pipeline(pool, body, prepare)


NAMES = ("x", "adj", *("L0_gnn_" + k for k in ("W", "a", "ln_g", "ln_b", "W1", "b1", "W2", "b2", "W3", "b3")),
         *("L0_ffn_" + k for k in ("Wr", "br", "W1", "b1", "g1", "be1", "m1", "v1", "W2", "b2", "g2", "be2", "m2",
                                   "v2", "Wo", "bo")))


def kernel(**inputs):
    import numpy as _np
    import concourse.bacc as _bacc
    from concourse import mybir as _mybir
    from concourse.bass_utils import run_bass_kernel_spmd as _run

    nc = _bacc.Bacc("TRN2", target_bir_lowering=False, num_devices=1)
    arrays, args = {}, []
    for name in NAMES:
        a = _np.ascontiguousarray(inputs[name])
        arrays[f"in_{name}_dram"] = a
        args.append(nc.dram_tensor(f"in_{name}_dram", a.shape, _mybir.dt.from_np(a.dtype), kind="ExternalInput").ap())
    args.append(nc.dram_tensor("out_0_dram", inputs["x"].shape, _mybir.dt.float32, kind="ExternalOutput").ap())
    build(nc, *args)
    return _run(nc, [arrays], core_ids=[0]).results[0]["out_0_dram"]
```

```python
from contextlib import ExitStack

import concourse.bass as bass
from concourse import mybir

ALU = mybir.AluOpType
ACT = mybir.ActivationFunctionType
AX = mybir.AxisListType.X
F32 = mybir.dt.float32
F16 = mybir.dt.float16

P = 128
ALPHA = 0.2
MLP_ALPHA = 0.01
LN_EPS = 1e-5
BN_EPS = 1e-3
X_BOUND = 11.4
K1 = 2.0 ** 8
K2 = 2.0 ** 14
K3 = 2.0 ** 13


def build(nc, x, adj, W, a, ln_g, ln_b, W1, b1, W2, b2, W3, b3, Wr, br,
          E1, c1, g1, be1, m1, v1, E2, c2, g2, be2, m2, v2, Eo, bo, out):
    NB, S, D = x.shape
    NE = E1.shape[0]
    C = 64
    T = S // P
    N = NB * P
    HALF = N // 2
    assert D == P and HALF == 512 and T % 2 == 0 and NE == 8

    x_t = x.rearrange("b (t p) d -> t p b d", p=P)
    out_t = out.rearrange("b (t p) d -> t p b d", p=P)
    adj_t = adj.rearrange("b (t k i) (u l j) -> t k u l i b j", k=2, i=C, l=2, j=C)

    with ExitStack() as ctx:
        def sb(name, shape, dt=F32):
            return ctx.enter_context(nc.sbuf_tensor(name, shape, dt))

        def psum(name, shape):
            return ctx.enter_context(nc.psum_tensor(name, shape, F32))

        def sem(name):
            return ctx.enter_context(nc.semaphore(name))

        ident = sb("ident", [P, P])
        ones = sb("ones", [P, P])
        neg_half = sb("neg_half", [P, 2 * NE])
        same_e = sb("same_e", [P, NE * NE])
        pick = sb("pick", [2 * NE, NE])
        spread = sb("spread", [2 * NE, NE, P], F16)
        w_sb = sb("w_sb", [P, P])
        w1_sb = sb("w1_sb", [P, P])
        w2_sb = sb("w2_sb", [P, P])
        w3_sb = sb("w3_sb", [P, P])
        wt_sb = sb("wt_sb", [P, P])
        ww1_sb = sb("ww1_sb", [P, P])
        a_col = sb("a_col", [P, 1])
        a_wide = sb("a_wide", [P, P])
        wa_wide = sb("wa_wide", [P, P])
        b1_col = sb("b1_col", [P, 1])
        b2_col = sb("b2_col", [P, 1])
        b3_wide = sb("b3_wide", [P, P])
        lng = sb("lng", [P, P])
        lnb = sb("lnb", [P, P])
        wr_sb = sb("wr_sb", [P, NE])
        br_sb = sb("br_sb", [P, NE])
        e1_hi = sb("e1_hi", [P, NE, P], F16)
        e1_lo = sb("e1_lo", [P, NE, P], F16)
        e2_hi = sb("e2_hi", [P, NE, P], F16)
        e2_lo = sb("e2_lo", [P, NE, P], F16)
        eo_hi = sb("eo_hi", [P, NE, P], F16)
        eo_lo = sb("eo_lo", [P, NE, P], F16)
        bo_row = sb("bo_row", [NE, P])
        bn_rows = sb("bn_rows", [5 * 2 * NE, P])
        bn_cols = sb("bn_cols", [P, 5, 2, NE])
        g_col, v_col, m_col, b_col, c_col = (bn_cols[:, i, :, :] for i in range(5))
        s_col = sb("s_col", [P, 2, NE])
        t_col = sb("t_col", [P, 2, NE])
        s_abs = sb("s_abs", [P, 2, NE])
        t_abs = sb("t_abs", [P, 2, NE])
        t2_diag = sb("t2_diag", [P, NE, NE])
        iu_col = sb("iu_col", [P, 2, NE])
        u_col = sb("u_col", [P, 2, NE])
        su_col = sb("su_col", [P, 2, NE])
        bias1 = sb("bias1", [P, NE])
        neg_bias2 = sb("neg_bias2", [P, NE])
        iuo_col = sb("iuo_col", [P, 1])
        uo_col = sb("uo_col", [P, 1])
        uo_diag = sb("uo_diag", [P, P])
        c_row = sb("c_row", [NE, P])
        x_in = [sb(f"x_in{i}", [P, NB, P]) for i in range(2)]
        adj_in = [sb(f"adj_in{i}", [P, NB, C]) for i in range(2)]
        stat_a = sb("stat_a", [P, NB, 6])
        mean2_a = sb("mean2_a", [P, NB])
        gap_a = sb("gap_a", [P, NB])
        ve_a = sb("ve_a", [P, NB])
        rstd_a = sb("rstd_a", [P, NB])
        shift_a = sb("shift_a", [P, NB])
        xn = [sb(f"xn{i}", [P, NB, P]) for i in range(2)]
        xn_wa = sb("xn_wa", [P, NB, P])
        factor = sb("factor", [P, NB])
        scores = sb("scores", [P, NB, C])
        top = sb("top", [P, NB])
        total = sb("total", [P, NB])
        inv_total = sb("inv_total", [P, NB])
        probs = [sb(f"probs{i}", [P, NB, 2, C]) for i in range(2)]
        probs_t = sb("probs_t", [P, NB, P])
        mix = sb("mix", [P, N])
        mlp1 = sb("mlp1", [P, N])
        mlp2 = sb("mlp2", [P, N])
        z = sb("z", [P, NB, P])
        stat_b = sb("stat_b", [P, NB, 6])
        mean2_b = sb("mean2_b", [P, NB])
        gap_b = sb("gap_b", [P, NB])
        ve_b = sb("ve_b", [P, NB])
        rstd_b = sb("rstd_b", [P, NB])
        shift_b = sb("shift_b", [P, NB])
        xb = sb("xb", [P, NB, P])
        x1 = [sb(f"x1_{i}", [P, NB, P]) for i in range(2)]
        stat_c = sb("stat_c", [P, NB, 6])
        mean2_c = sb("mean2_c", [P, NB])
        gap_c = sb("gap_c", [P, NB])
        ve_c = sb("ve_c", [P, NB])
        rstd_c = sb("rstd_c", [P, NB])
        shift_c = sb("shift_c", [P, NB])
        x1n = sb("x1n", [P, NB, P])
        sum4 = sb("sum4", [P, 4, P])
        sum2 = sb("sum2", [P, 2, P])
        feat = sb("feat", [P, P])
        feat_t = sb("feat_t", [P, P])
        logit = sb("logit", [P, NE])
        neg_top = sb("neg_top", [P, 1])
        ex = sb("ex", [P, NE])
        ex_sum = sb("ex_sum", [P, 1])
        ex_inv = sb("ex_inv", [P, 1])
        rw = sb("rw", [P, NE])
        rw16 = sb("rw16", [P, 2 * NE], F16)
        ident16 = sb("ident16", [P, P], F16)
        rw_t = sb("rw_t", [NE, P])
        rw16_t = sb("rw16_t", [2 * NE, P], F16)
        x_hi = [sb(f"x_hi{i}", [P, N], F16) for i in range(2)]
        x_lo = [sb(f"x_lo{i}", [P, N], F16) for i in range(2)]
        route = [sb(f"route{i}", [P, NE, P]) for i in range(2)]
        y_bias = sb("y_bias", [P, P])
        x1_kept = [sb(f"x1_kept{i}", [P, NB, P]) for i in range(2)]
        r1 = [sb(f"r1_{i}", [P, N]) for i in range(2)]
        h1_hi = [sb(f"h1_hi{i}", [P, N], F16) for i in range(2)]
        h1_lo = [sb(f"h1_lo{i}", [P, N], F16) for i in range(2)]
        h2_hi = [sb(f"h2_hi{i}", [P, N], F16) for i in range(2)]
        h2_lo = [sb(f"h2_lo{i}", [P, N], F16) for i in range(2)]
        r2 = sb("r2", [P, N])
        y_t = sb("y_t", [P, N])
        y_out = [sb(f"y_out{i}", [P, NB, P]) for i in range(2)]
        e1_sb = r1[0][:, :].rearrange("p (e h) -> p e h", e=NE)
        e2_sb = r1[1][:, :].rearrange("p (e h) -> p e h", e=NE)
        eo_sb = y_t[:, :].rearrange("p (e h) -> p e h", e=NE)
        abs_w = (*y_out, x1_kept[1])
        su_diag = (route[1][:, :, :], r2[:, :].rearrange("p (e h) -> p e h", e=NE))
        Z1 = psum("Z1", [P, N])
        Z2 = psum("Z2", [P, N])
        Y = psum("Y", [P, N])
        F = psum("F", [P, N])

        SUMS1, SUMS2, SUMS3 = Z2[:, 0:NE], Y[:, 0:NE], Z1[:, 0:1]
        UO_WIDE = Y[:, HALF:HALF + P]

        wa_landed = sem("wa_landed")
        gnn_landed = sem("gnn_landed")
        bn_landed = sem("bn_landed")
        experts_landed = [sem(f"experts{i}_landed") for i in range(3)]
        ident_zero = sem("ident_zero")
        ident_ready = sem("ident_ready")
        consts_ready = sem("consts_ready")
        same_zero = sem("same_zero")
        same_ready = sem("same_ready")
        probs_zero = sem("probs_zero")
        wt_done = sem("wt_done")
        wt_ready = sem("wt_ready")
        wa_done = sem("wa_done")
        a_wide_ready = sem("a_wide_ready")
        wa_ready = sem("wa_ready")
        ww1_done = sem("ww1_done")
        ww1_ready = sem("ww1_ready")
        pick_ready = sem("pick_ready")
        spread_ready = sem("spread_ready")
        ident16_ready = sem("ident16_ready")
        bn_turned = sem("bn_turned")
        bn_cols_ready = sem("bn_cols_ready")
        bn_var = sem("bn_var")
        bn_rstd = sem("bn_rstd")
        bn_step = sem("bn_step")
        t2_diag_ready = sem("t2_diag_ready")
        c_done = sem("c_done")
        c_ready = sem("c_ready")
        abs_ready = sem("abs_ready")
        sums_done = sem("sums_done")
        u_step = sem("u_step")
        iu_ready = sem("iu_ready")
        diag_ready = sem("diag_ready")
        wide_done = sem("wide_done")
        rows_scaled = sem("rows_scaled")
        scaled = sem("scaled")
        hi_ready = sem("hi_ready")
        lo_ready = sem("lo_ready")
        bias_ready = sem("bias_ready")
        x_landed = [sem(f"x_landed{i}") for i in range(2)]
        adj_landed = [sem(f"adj_landed{i}") for i in range(2)]
        y_out_free = [sem(f"y_out_free{i}") for i in range(2)]
        stat_a_done, halves_a_done = sem("stat_a_done"), sem("halves_a_done")
        terms_a_done, ve_a_done = sem("terms_a_done"), sem("ve_a_done")
        rstd_a_done, shift_a_done = sem("rstd_a_done"), sem("shift_a_done")
        stat_b_done, halves_b_done = sem("stat_b_done"), sem("halves_b_done")
        terms_b_done, ve_b_done = sem("terms_b_done"), sem("ve_b_done")
        rstd_b_done, shift_b_done = sem("rstd_b_done"), sem("shift_b_done")
        stat_c_done, halves_c_done = sem("stat_c_done"), sem("halves_c_done")
        terms_c_done, ve_c_done = sem("terms_c_done"), sem("ve_c_done")
        rstd_c_done, shift_c_done = sem("rstd_c_done"), sem("shift_c_done")
        mix_done = sem("mix_done")
        probs_turned, mlp1_done = sem("probs_turned"), sem("mlp1_done")
        mlp2_done, z_done = sem("mlp2_done"), sem("z_done")
        x1n_turned, feat_turned, router_done = sem("x1n_turned"), sem("feat_turned"), sem("router_done")
        rw_turned, route_done, y_bias_done = sem("rw_turned"), sem("route_done"), sem("y_bias_done")
        y_turned = sem("y_turned")
        xn_ready = sem("xn_ready")
        xn_wa_ready = sem("xn_wa_ready")
        factor_sum_done = sem("factor_sum_done")
        leaky_done = sem("leaky_done")
        weighed = sem("weighed")
        top_done = sem("top_done")
        lowered = sem("lowered")
        exp_done = sem("exp_done")
        total_done = sem("total_done")
        inv_total_done = sem("inv_total_done")
        probs_ready = sem("probs_ready")
        probs_t_ready = sem("probs_t_ready")
        mix_ready = sem("mix_ready")
        mlp1_linear = sem("mlp1_linear")
        mlp1_ready = sem("mlp1_ready")
        mlp2_linear = sem("mlp2_linear")
        mlp2_ready = sem("mlp2_ready")
        z_ready = sem("z_ready")
        z_normed = sem("z_normed")
        z_gained = sem("z_gained")
        xb_ready = sem("xb_ready")
        x1_ready = sem("x1_ready")
        x1_kept_ready = sem("x1_kept_ready")
        x1n_ready = sem("x1n_ready")
        sum4_done, sum2_done, feat_done = sem("sum4_done"), sem("sum2_done"), sem("feat_done")
        x_hi_ready = sem("x_hi_ready")
        x_lo_ready = sem("x_lo_ready")
        feat_t_ready = sem("feat_t_ready")
        logit_ready = sem("logit_ready")
        neg_top_done = sem("neg_top_done")
        ex_done = sem("ex_done")
        ex_inv_done = sem("ex_inv_done")
        rw_ready = sem("rw_ready")
        rw_hi_ready = sem("rw_hi_ready")
        rw16_ready = sem("rw16_ready")
        rw_t_ready = sem("rw_t_ready")
        rw16_t_ready = sem("rw16_t_ready")
        route_ready = sem("route_ready")
        y_bias_ready = sem("y_bias_ready")
        z1_done = sem("z1_done")
        r1_ready = sem("r1_ready")
        h1_hi_ready = sem("h1_hi_ready")
        h1_lo_ready = sem("h1_lo_ready")
        z2_done = sem("z2_done")
        r2_ready = sem("r2_ready")
        h2_hi_ready = sem("h2_hi_ready")
        h2_lo_ready = sem("h2_lo_ready")
        y_done = sem("y_done")
        y_t_ready = sem("y_t_ready")
        y_out_ready = sem("y_out_ready")

        WA_LOADS = [(w_sb[:, :], W), (a_col[:, :], a)]
        GNN_LOADS = [(w1_sb[:, :], W1), (w2_sb[:, :], W2), (w3_sb[:, :], W3),
                     (b1_col[:, :], b1.rearrange("(p o) -> p o", o=1)),
                     (b2_col[:, :], b2.rearrange("(p o) -> p o", o=1)),
                     (b3_wide[:, :], b3.partition_broadcast(P)),
                     (lng[:, :], ln_g.partition_broadcast(P)), (lnb[:, :], ln_b.partition_broadcast(P)),
                     (wr_sb[:, :], Wr), (br_sb[:, :], br.partition_broadcast(P)), (bo_row[:, :], bo)]
        BN_LOADS = [(bn_rows[i * NE:(i + 1) * NE, :], src)
                    for i, src in enumerate((g1, g2, v1, v2, m1, m2, be1, be2, c1, c2))]
        EXPERT_LOADS = [(e1_sb[:, :, :], E1.rearrange("e d h -> d e h")),
                        (e2_sb[:, :, :], E2.rearrange("e d h -> d e h")),
                        (eo_sb[:, :, :], Eo.rearrange("e d h -> d e h"))]
        PREPARE = {(-3, 4): 0, (-3, 6): 1, (-2, 0): 2, (-2, 1): 3, (-2, 3): 4, (-2, 5): 5}

        def wait(eng, s, count):
            if not (isinstance(count, int) and count <= 0):
                eng.wait_ge(s, count)

        def pipeline(eng, body):
            for n in range(-4, 1):
                body(0, n)
            with eng.Fori(0, (T - 6) // 2) as u:
                body(u, 1)
                body(u, 2)
            for n in range(T - 5, T + 1):
                body(0, n)

        def parts(u, c):
            n = 2 * u + c
            if not isinstance(n, int):
                return n, True, True, True, True, True, True
            return (n, *(0 <= n + k < T for k in (0, 1, 2, 3, 4, -1)))

        def flat(t):
            return t[:, :, :].rearrange("p b d -> p (b d)")

        block = ctx.enter_context(nc.Block())

        @block.sync
        def _(sp):
            def load(u, c):
                t = 2 * u + c
                wait(sp, xn_ready, t - 1)
                wait(sp, xb_ready, t - 1)
                sp.dma_start(x_in[c % 2][:, :, :], x_t[t]).then_inc(x_landed[c % 2], 16)
                if isinstance(t, int) and t == 0:
                    for dst, src in WA_LOADS:
                        sp.dma_start(dst, src).then_inc(wa_landed, 16)
                wait(sp, weighed, t - 1)
                for k in range(2):
                    sp.dma_start(adj_in[c % 2][k * C:(k + 1) * C, :, :],
                                 adj_t[t, k, t, k]).then_inc(adj_landed[c % 2], 16)

            for i in range(2):
                sp.sem_inc(y_out_free[i], 16)
            load(0, 0)
            for dst, src in GNN_LOADS:
                sp.dma_start(dst, src).then_inc(gnn_landed, 16)
            load(0, 1)

            def body(u, c):
                n, ffn, has_c, has_b, has_a, has_next, last = parts(u, c)
                if has_next and not (isinstance(n, int) and n <= -3):
                    load(u, c + 4)
                if last:
                    sp.wait_ge(y_out_ready, n)
                    sp.dma_start(out_t[n - 1], y_out[(c - 1) % 2][:, :, :]).then_inc(y_out_free[(c - 1) % 2], 16)

            pipeline(sp, body)
            for i in range(2):
                sp.wait_ge(y_out_free[i], 16 * (T // 2 + 1))

        @block.tensor
        def _(pe):
            def products(dst, hi, lo, m_hi, m_lo, first, last, lo_ready=None):
                for k, (w, m) in enumerate(((hi, m_hi), (lo, m_hi), (hi, m_lo))):
                    if k == 2 and lo_ready is not None:
                        pe.wait_ge(*lo_ready)
                    for j in range(2):
                        cols = slice(j * HALF, (j + 1) * HALF)
                        mm = pe.matmul(dst[:, cols], w, m[:, cols], start=(first and k == 0), stop=(last and k == 2))
                return mm

            def turn(src):
                for b in range(NB):
                    mm = pe.transpose(F[:, b * P:(b + 1) * P], src[:, b * P:(b + 1) * P], ident[:, :])
                return mm

            def wide(w, src):
                for j in range(2):
                    cols = slice(j * HALF, (j + 1) * HALF)
                    mm = pe.matmul(F[:, cols], w, src[:, cols], start=True, stop=True)
                return mm

            def mlp_and_attention(b0, b1):
                for b in range(b0, b1):
                    cols = slice(b * P, (b + 1) * P)
                    pe.matmul(F[:, cols], mlp2[:, cols], w3_sb[:, :], start=True, stop=False)
                    mm = pe.matmul(F[:, cols], mix[:, cols], w_sb[:, :], start=False, stop=True)
                return mm

            pe.wait_ge(ident_ready, 1)
            pe.wait_ge(wa_landed, 16 * len(WA_LOADS))
            pe.transpose(F[:, 0:P], w_sb[:, :], ident[:, :]).then_inc(wt_done, 1)
            pe.wait_ge(wt_ready, 1)
            pe.wait_ge(a_wide_ready, 1)
            pe.matmul(F[:, HALF:HALF + P], a_wide[:, :], wt_sb[:, :], start=True, stop=True).then_inc(wa_done, 1)
            pe.wait_ge(gnn_landed, 16 * len(GNN_LOADS))
            pe.matmul(F[:, 0:P], wt_sb[:, :], w1_sb[:, :], start=True, stop=True).then_inc(ww1_done, 1)

            def prepare(step):
                def wide_u(dst, diag):
                    for j in range(2):
                        mm = pe.matmul(dst[:, j * HALF:(j + 1) * HALF], ones[:, :], diag[:, 4 * j:4 * j + 4, :],
                                       start=True, stop=True)
                    mm.then_inc(wide_done, 1)

                if step == 0:
                    pe.wait_ge(bn_landed, 16 * len(BN_LOADS))
                    pe.transpose(Y[:, 0:5 * 2 * NE], bn_rows[:, :], ident[0:5 * 2 * NE, 0:5 * 2 * NE]
                                 ).then_inc(bn_turned, 1)
                if step == 1:
                    pe.wait_ge(consts_ready, 1)
                    pe.wait_ge(abs_ready, 1)
                    for e in range(NE):
                        mm = pe.matmul(SUMS1[:, e:e + 1], abs_w[0][:, e, :], ones[:, 0:1], start=True, stop=True)
                    mm.then_inc(sums_done, 1)
                if step == 2:
                    pe.wait_ge(t2_diag_ready, 1)
                    pe.wait_ge(experts_landed[2], 16)
                    for e in range(NE):
                        mm = pe.matmul(Y[0:NE, HALF:HALF + P], t2_diag[:, e, :], eo_sb[:, e, :],
                                       start=(e == 0), stop=(e == NE - 1))
                    mm.then_inc(c_done, 1)
                    pe.wait_ge(diag_ready, 1)
                    wide_u(Z1, su_diag[0])
                if step == 3:
                    pe.wait_ge(abs_ready, 2)
                    pe.wait_ge(iu_ready, 1)
                    for e in range(NE):
                        mm = pe.matmul(SUMS2[:, e:e + 1], abs_w[1][:, e, :], iu_col[:, 0, e:e + 1], start=True, stop=True)
                    mm.then_inc(sums_done, 1)
                if step == 4:
                    pe.wait_ge(diag_ready, 2)
                    wide_u(Z2, su_diag[1])
                    pe.wait_ge(abs_ready, 3)
                    for e in range(NE):
                        mm = pe.matmul(SUMS3[:, 0:1], abs_w[2][:, e, :], iu_col[:, 1, e:e + 1],
                                       start=(e == 0), stop=(e == NE - 1))
                    mm.then_inc(sums_done, 1)
                if step == 5:
                    pe.wait_ge(diag_ready, 3)
                    pe.matmul(UO_WIDE[:, :], ones[:, :], uo_diag[:, :], start=True, stop=True).then_inc(wide_done, 1)

            read_out = [(ww1_ready, 1)]

            def body(u, c):
                n, ffn, has_c, has_b, has_a, has_next, last = parts(u, c)
                if not isinstance(n, int) or n == T - 5:
                    read_out[0] = (route_ready, n + 1)

                def claim(then, count):
                    pe.wait_ge(*read_out[0])
                    read_out[0] = (then, count)

                def front(gap):
                    m = n + 2
                    if gap == 0 and has_b:
                        claim(probs_t_ready, m + 1)
                        pe.wait_ge(probs_ready, m + 1)
                        turn(probs[c % 2][:, :, :, :].rearrange("p b k j -> p (b k j)")).then_inc(probs_turned, 1)
                    if gap == 2 and has_b:
                        claim(mix_ready, m + 1)
                        pe.wait_ge(probs_t_ready, m + 1)
                        for b in range(NB):
                            mm = pe.matmul(F[:, b * P:(b + 1) * P], xn[c % 2][:, b, :], probs_t[:, b, :],
                                           start=True, stop=True)
                        mm.then_inc(mix_done, 1)
                    if gap == 4 and has_b:
                        claim(mlp1_linear, m + 1)
                        pe.wait_ge(mix_ready, m + 1)
                        wide(ww1_sb[:, :], mix).then_inc(mlp1_done, 1)
                    if gap == 9 and has_b:
                        claim(mlp2_linear, m + 1)
                        pe.wait_ge(mlp1_ready, m + 1)
                        wide(w2_sb[:, :], mlp1).then_inc(mlp2_done, 1)
                    if gap == 12 and has_b:
                        claim(z_ready, m + 1)
                        pe.wait_ge(mlp2_ready, m + 1)
                        mlp_and_attention(0, NB // 2)
                    if gap == 13 and has_b:
                        mlp_and_attention(NB // 2, NB).then_inc(z_done, 1)
                    m = n + 1
                    if gap == 10 and has_c:
                        claim(x_lo_ready, m + 1)
                        pe.wait_ge(x1n_ready, m + 1)
                        turn(flat(x1n)).then_inc(x1n_turned, 1)
                    if gap == 14 and has_c:
                        claim(feat_t_ready, m + 1)
                        pe.wait_ge(feat_done, m + 1)
                        pe.transpose(F[:, 0:P], feat[:, :], ident[:, :]).then_inc(feat_turned, 1)
                    if gap == 15 and has_c:
                        claim(logit_ready, m + 1)
                        pe.wait_ge(feat_t_ready, m + 1)
                        pe.matmul(F[:, 0:NE], feat_t[:, :], wr_sb[:, :], start=True, stop=True).then_inc(router_done, 1)
                    if gap == 20 and has_c:
                        claim(rw16_t_ready, m + 1)
                        pe.wait_ge(rw16_ready, m + 1)
                        if isinstance(n, int) and n == -1:
                            pe.wait_ge(ident16_ready, 1)
                        pe.transpose(F[0:NE, 0:P], rw[:, :], ident[:, :])
                        pe.transpose(F[0:2 * NE, HALF:HALF + P // 2].bitcast(F16), rw16[:, :],
                                     ident16[:, :]).then_inc(rw_turned, 1)
                    if gap == 22 and has_c:
                        claim(route_ready, m + 1)
                        if isinstance(n, int) and n == -1:
                            pe.wait_ge(spread_ready, 1)
                        for e in range(NE):
                            mm = pe.matmul(F[:, e * P:(e + 1) * P], spread[:, e, :], rw16_t[:, :],
                                           start=True, stop=True)
                        mm.then_inc(route_done, 1)
                    if gap == 17 and ffn:
                        claim(y_bias_ready, n + 1)
                        if isinstance(n, int) and n == 0:
                            pe.wait_ge(c_ready, 1)
                        pe.wait_ge(rw_t_ready, n + 1)
                        pe.matmul(F[:, 0:P], c_row[:, :], rw_t[:, :], start=True, stop=True).then_inc(y_bias_done, 1)
                    if gap == 7 and last:
                        claim(y_out_ready, n)
                        pe.wait_ge(y_t_ready, n)
                        turn(y_t).then_inc(y_turned, 1)

                for e in range(NE):
                    g = NE * n + e
                    if ffn:
                        if isinstance(n, int) and n == 0 and e == 0:
                            pe.wait_ge(lo_ready, 3)
                        if e == 0:
                            pe.wait_ge(x_hi_ready, n + 1)
                        wait(pe, r1_ready, g)
                        products(Z1, e1_hi[:, e, :], e1_lo[:, e, :], x_hi[c % 2], x_lo[c % 2], True, True,
                                 (x_lo_ready, n + 1) if e == 0 else None).then_inc(z1_done, 1)
                    front(3 * e)
                    if (ffn and not (isinstance(g, int) and g == 0)) or (not ffn and last and e == 0):
                        k = (e - 1) % NE
                        wait(pe, r2_ready, g - 1)
                        pe.wait_ge(h1_hi_ready, g)
                        products(Z2, e2_hi[:, k, :], e2_lo[:, k, :], h1_hi[k % 2], h1_lo[k % 2],
                                 True, True, (h1_lo_ready, g)).then_inc(z2_done, 1)
                    front(3 * e + 1)
                    if (ffn and not (isinstance(g, int) and g <= 1)) or (not ffn and last and e <= 1):
                        k = (e - 2) % NE
                        pe.wait_ge(h2_hi_ready, g - 1)
                        if k == 0:
                            wait(pe, y_t_ready, n)
                        products(Y, eo_hi[:, k, :], eo_lo[:, k, :], h2_hi[k % 2], h2_lo[k % 2], k == 0, k == NE - 1,
                                 (h2_lo_ready, g - 1)).then_inc(y_done, 1)
                    front(3 * e + 2)
                    if isinstance(n, int) and (n, e) in PREPARE:
                        prepare(PREPARE[n, e])

            pipeline(pe, body)

        @block.scalar
        def _(act):
            for (dst, src), landed in zip(EXPERT_LOADS, experts_landed):
                act.dma_start(dst, src).then_inc(landed, 16)
            for dst, src in BN_LOADS:
                act.dma_start(dst, src).then_inc(bn_landed, 16)

            def prepare(step):
                WEIGHTS = (e1_sb, e2_sb, eo_sb)
                if step == 0:
                    for w, dst, landed in zip(WEIGHTS, abs_w, experts_landed):
                        act.wait_ge(landed, 16)
                        act.activation(dst[:, :, :], w[:, :, :], ACT.Abs).then_inc(abs_ready, 1)
                layer = {2: 0, 4: 1, 5: 2}.get(step)
                if layer is not None:
                    act.wait_ge(scaled, layer + 1)
                    act.activation((e1_hi, e2_hi, eo_hi)[layer][:, :, :], WEIGHTS[layer][:, :, :],
                                   ACT.Copy).then_inc(hi_ready, 1)

            def body(u, c):
                n, ffn, has_c, has_b, has_a, has_next, last = parts(u, c)

                def front(e, place):
                    at = (e, place)
                    m = n + 2
                    if at == (0, 0) and has_b:
                        act.wait_ge(probs_turned, m + 1)
                        wait(act, mix_done, m)
                        act.activation(flat(probs_t), F[:, :], ACT.Copy).then_inc(probs_t_ready, 1)
                    if at == (0, 2) and has_b:
                        act.wait_ge(mix_done, m + 1)
                        wait(act, z_done, m)
                        act.activation(mix[:, :], F[:, :], ACT.Copy).then_inc(mix_ready, 1)
                    if at == (1, 1) and has_b:
                        act.wait_ge(mlp1_done, m + 1)
                        wait(act, mlp2_done, m)
                        act.activation(mlp1[:, :], F[:, :], ACT.Identity, bias=b1_col[:, 0:1]).then_inc(mlp1_linear, 1)
                    if at == (3, 0) and has_b:
                        act.wait_ge(mlp2_done, m + 1)
                        wait(act, z_done, m)
                        act.activation(mlp2[:, :], F[:, :], ACT.Identity, bias=b2_col[:, 0:1]).then_inc(mlp2_linear, 1)
                    pieces = {(6, 1): (0, 3), (6, 2): (3, 6), (7, 0): (6, NB)}.get(at)
                    if pieces and has_b:
                        if pieces[0] == 0:
                            act.wait_ge(shift_b_done, m + 1)
                        for b in range(*pieces):
                            i = act.activation(z[:, b, :], z[:, b, :], ACT.Identity,
                                               bias=shift_b[:, b:b + 1], scale=rstd_b[:, b:b + 1])
                        if pieces[1] == NB:
                            i.then_inc(z_normed, 1)
                    m = n + 3
                    pieces = {(0, 1): (0, 2), (0, 2): (2, 4), (1, 2): (4, 6), (2, 0): (6, NB)}.get(at)
                    if pieces and has_a:
                        if pieces[0] == 0:
                            act.wait_ge(shift_a_done, m + 1)
                            wait(act, mix_done, m - 1)
                        for b in range(*pieces):
                            i = act.activation(xn[(c + 3) % 2][:, b, :], x_in[(c + 3) % 2][:, b, :], ACT.Identity,
                                               bias=shift_a[:, b:b + 1], scale=rstd_a[:, b:b + 1])
                        if pieces[1] == NB:
                            i.then_inc(xn_ready, 1)
                    if at == (5, 1) and has_a:
                        act.wait_ge(lowered, m + 1)
                        act.activation(scores[:, :, :], scores[:, :, :], ACT.Exp).then_inc(exp_done, 1)
                    m = n + 1
                    if at == (3, 1) and has_c:
                        act.wait_ge(x1n_turned, m + 1)
                        wait(act, z1_done, NE * (m - 1))
                        act.activation(x_hi[(c + 1) % 2][:, :], F[:, :], ACT.Copy).then_inc(x_hi_ready, 1)
                    if at == (4, 2) and has_c:
                        act.wait_ge(feat_turned, m + 1)
                        wait(act, router_done, m)
                        act.activation(feat_t[:, :], F[:, 0:P], ACT.Copy, scale=1.0 / NB).then_inc(feat_t_ready, 1)
                    if at == (6, 0) and has_c:
                        act.wait_ge(neg_top_done, m + 1)
                        act.activation(ex[:, :], logit[:, :], ACT.Exp, bias=neg_top[:, 0:1],
                                       accum_out=ex_sum[:, 0:1]).then_inc(ex_done, 1)
                    if at == (6, 2) and has_c:
                        act.wait_ge(rw_turned, m + 1)
                        wait(act, y_bias_done, m)
                        act.activation(rw_t[:, :], F[0:NE, 0:P], ACT.Copy).then_inc(rw_t_ready, 1)
                        act.activation(rw16_t[:, :], F[0:2 * NE, HALF:HALF + P // 2].bitcast(F16),
                                       ACT.Copy).then_inc(rw16_t_ready, 1)
                    if at == (7, 1) and has_c:
                        act.wait_ge(route_done, m + 1)
                        wait(act, r2_ready, NE * (m - 1))
                        act.activation(flat(route[(c + 1) % 2]), F[:, :], ACT.Copy).then_inc(route_ready, 1)
                    if at == (5, 2) and ffn:
                        act.wait_ge(y_bias_done, n + 1)
                        wait(act, y_t_ready, n)
                        act.activation(y_bias[:, :], F[:, 0:P], ACT.Copy).then_inc(y_bias_ready, 1)

                for e in range(NE):
                    g = NE * n + e
                    i = e % 2
                    if ffn:
                        if isinstance(n, int) and n == 0 and e == 0:
                            act.wait_ge(bias_ready, 1)
                        act.wait_ge(z1_done, g + 1)
                        wait(act, h1_lo_ready, g - 1)
                        act.activation(r1[i][:, :], Z1[:, :], ACT.Relu, bias=bias1[:, e:e + 1]).then_inc(r1_ready, 1)
                    front(e, 0)
                    if ffn:
                        act.wait_ge(r1_ready, g + 1)
                        wait(act, z2_done, g - 1)
                        act.activation(h1_hi[i][:, :], r1[i][:, :], ACT.Copy).then_inc(h1_hi_ready, 1)
                    front(e, 1)
                    if (ffn and not (isinstance(g, int) and g == 0)) or (not ffn and last and e == 0):
                        act.wait_ge(r2_ready, g)
                        wait(act, y_done, g - 2)
                        act.activation(h2_hi[1 - i][:, :], r2[:, :], ACT.Copy).then_inc(h2_hi_ready, 1)
                    front(e, 2)
                    if isinstance(n, int) and (n, e) in PREPARE:
                        prepare(PREPARE[n, e])

            pipeline(act, body)

        @block.vector
        def _(dve):
            def token_stats(stat, src, b0, b1, stat_done=None):
                for b in range(b0, b1):
                    i = dve.bn_stats(stat[:, b, :], src[:, b, :])
                if stat_done is not None:
                    i.then_inc(stat_done, 1)

            def norm_stats(tiles, sems, m):
                stat, mean2, gap, ve = tiles
                stat_done, halves_done, terms_done, ve_done = sems
                dve.wait_ge(stat_done, m + 1)
                dve.tensor_tensor(gap[:, :], stat[:, :, 1], stat[:, :, 4], ALU.subtract)
                dve.tensor_tensor(ve[:, :], stat[:, :, 2], stat[:, :, 5], ALU.add)
                dve.tensor_tensor(mean2[:, :], stat[:, :, 1], stat[:, :, 4], ALU.add).then_inc(halves_done, 1)
                dve.wait_ge(halves_done, m + 1)
                dve.scalar_tensor_tensor(gap[:, :], gap[:, :], 0.25, gap[:, :], ALU.mult, ALU.mult)
                dve.tensor_scalar(ve[:, :], ve[:, :], 1.0 / D, LN_EPS, ALU.mult, ALU.add).then_inc(terms_done, 1)
                dve.wait_ge(terms_done, m + 1)
                dve.tensor_tensor(ve[:, :], ve[:, :], gap[:, :], ALU.add).then_inc(ve_done, 1)

            def norm_shift(shift, mean2, rstd, rstd_done, shift_done, m):
                dve.wait_ge(rstd_done, m + 1)
                dve.scalar_tensor_tensor(shift[:, :], mean2[:, :], -0.5, rstd[:, :], ALU.mult,
                                         ALU.mult).then_inc(shift_done, 1)

            def leaky(h, linear, ready, m):
                dve.wait_ge(linear, m + 1)
                dve.scalar_tensor_tensor(h[:, :], h[:, :], MLP_ALPHA, h[:, :], ALU.mult, ALU.max).then_inc(ready, 1)

            def over_heads(col, like):
                return col[:, :].unsqueeze(2).broadcast_to([P, NB, like])

            def scales(layer, sums, in_bound, out_bound):
                iu, su = iu_col[:, layer, :], su_col[:, layer, :]
                dve.wait_ge(sums_done, layer + 1)
                dve.scalar_tensor_tensor(iu, sums, in_bound / out_bound, s_abs[:, layer, :], ALU.mult,
                                         ALU.mult).then_inc(u_step, 1)
                dve.wait_ge(u_step, 4 * layer + 1)
                dve.scalar_tensor_tensor(iu, t_abs[:, layer, :], 1.0 / out_bound, iu, ALU.mult,
                                         ALU.add).then_inc(u_step, 1)
                dve.wait_ge(u_step, 4 * layer + 2)
                dve.tensor_scalar(iu, iu, 1e-30, None, ALU.max).then_inc(iu_ready, 1)
                dve.wait_ge(iu_ready, layer + 1)
                dve.reciprocal(u_col[:, layer, :], iu).then_inc(u_step, 1)
                dve.wait_ge(u_step, 4 * layer + 3)
                dve.tensor_tensor(su, s_col[:, layer, :], u_col[:, layer, :], ALU.mult).then_inc(u_step, 1)
                dve.wait_ge(u_step, 4 * layer + 4)
                dve.tensor_tensor(su_diag[layer], ident[:, :].unsqueeze(1).broadcast_to([P, NE, P]),
                                  su.unsqueeze(2).broadcast_to([P, NE, P]), ALU.mult).then_inc(diag_ready, 1)

            def constants():
                dve.wait_ge(consts_ready, 1)
                dve.wait_ge(wa_landed, 16 * len(WA_LOADS))
                dve.tensor_scalar(a_wide[:, :], ones[:, :], a_col[:, 0:1], None, ALU.mult).then_inc(a_wide_ready, 1)
                dve.wait_ge(wt_done, 1)
                dve.tensor_copy(wt_sb[:, :], F[:, 0:P]).then_inc(wt_ready, 1)
                dve.wait_ge(wa_done, 1)
                dve.tensor_copy(wa_wide[:, :], F[:, HALF:HALF + P]).then_inc(wa_ready, 1)
                dve.wait_ge(ww1_done, 1)
                dve.tensor_copy(ww1_sb[:, :], F[:, 0:P]).then_inc(ww1_ready, 1)

            def prepare(step):
                if step == 0:
                    dve.wait_ge(bn_turned, 1)
                    dve.tensor_copy(bn_cols[:, :, :, :].rearrange("p k l e -> p (k l e)"),
                                    Y[:, 0:5 * 2 * NE]).then_inc(bn_cols_ready, 1)
                    dve.wait_ge(bn_cols_ready, 1)
                    dve.tensor_scalar(v_col, v_col, BN_EPS, None, ALU.add).then_inc(bn_var, 1)
                    dve.tensor_tensor(t_col[:, :, :], c_col, m_col, ALU.subtract).then_inc(bn_step, 1)
                if step == 1:
                    dve.wait_ge(bn_rstd, 1)
                    dve.tensor_tensor(s_col[:, :, :], g_col, v_col, ALU.mult).then_inc(bn_step, 1)
                    dve.wait_ge(bn_step, 2)
                    dve.tensor_tensor(t_col[:, :, :], t_col[:, :, :], s_col[:, :, :], ALU.mult).then_inc(bn_step, 1)
                    dve.scalar_tensor_tensor(s_abs[:, :, :], s_col[:, :, :], -1.0, s_col[:, :, :], ALU.mult, ALU.max)
                    dve.wait_ge(bn_step, 3)
                    dve.tensor_tensor(t_col[:, :, :], t_col[:, :, :], b_col, ALU.add).then_inc(bn_step, 1)
                    dve.wait_ge(bn_step, 4)
                    dve.scalar_tensor_tensor(t_abs[:, :, :], t_col[:, :, :], -1.0, t_col[:, :, :], ALU.mult,
                                             ALU.max).then_inc(bn_step, 1)
                    dve.wait_ge(same_ready, 1)
                    dve.tensor_tensor(t2_diag[:, :, :], same_e[:, :].rearrange("p (e f) -> p e f", f=NE),
                                      t_col[:, 1, :].unsqueeze(2).broadcast_to([P, NE, NE]), ALU.mult
                                      ).then_inc(t2_diag_ready, 1)
                    dve.wait_ge(bn_step, 5)
                    scales(0, SUMS1, X_BOUND, K1)
                if step == 2:
                    dve.wait_ge(c_done, 1)
                    dve.wait_ge(gnn_landed, 16 * len(GNN_LOADS))
                    dve.tensor_tensor(c_row[:, :], Y[0:NE, HALF:HALF + P], bo_row[:, :], ALU.add).then_inc(c_ready, 1)
                    dve.wait_ge(wide_done, 1)
                    dve.wait_ge(abs_ready, 1)
                    dve.tensor_tensor(flat(e1_sb), flat(e1_sb), Z1[:, :], ALU.mult).then_inc(scaled, 1)
                if step == 3:
                    dve.wait_ge(ident_ready, 1)
                    dve.tensor_tensor(pick[:, :], ident[0:2 * NE, 0:NE], ident[0:2 * NE, NE:2 * NE],
                                      ALU.add).then_inc(pick_ready, 1)
                    dve.wait_ge(pick_ready, 1)
                    dve.tensor_copy(spread[:, :, :], pick[:, :].unsqueeze(2).broadcast_to([2 * NE, NE, P])
                                    ).then_inc(spread_ready, 1)
                    dve.tensor_copy(ident16[:, :], ident[:, :]).then_inc(ident16_ready, 1)
                    scales(1, SUMS2, K1, K2)
                if step == 4:
                    dve.wait_ge(wide_done, 2)
                    dve.wait_ge(rows_scaled, 1)
                    dve.tensor_tensor(flat(e2_sb), flat(e2_sb), Z2[:, :], ALU.mult).then_inc(scaled, 1)
                    dve.tensor_tensor(bias1[:, :], t_col[:, 0, :], u_col[:, 0, :], ALU.mult)
                    dve.scalar_tensor_tensor(neg_bias2[:, :], t_col[:, 1, :], -1.0, u_col[:, 1, :], ALU.mult,
                                             ALU.mult).then_inc(bias_ready, 1)
                if step == 5:
                    dve.wait_ge(sums_done, 3)
                    dve.tensor_scalar(iuo_col[:, :], SUMS3, 1.0 / K3, 1e-30, ALU.mult, ALU.max).then_inc(iu_ready, 1)
                    dve.wait_ge(iu_ready, 3)
                    dve.reciprocal(uo_col[:, :], iuo_col[:, :]).then_inc(u_step, 1)
                    dve.wait_ge(u_step, 9)
                    dve.tensor_scalar(uo_diag[:, :], ident[:, :], uo_col[:, 0:1], None, ALU.mult).then_inc(diag_ready, 1)
                    dve.wait_ge(wide_done, 3)
                    dve.wait_ge(rows_scaled, 2)
                    dve.tensor_tensor(eo_sb[:, :, :], eo_sb[:, :, :], UO_WIDE.unsqueeze(1).broadcast_to([P, NE, P]),
                                      ALU.mult).then_inc(scaled, 1)

            def body(u, c):
                n, ffn, has_c, has_b, has_a, has_next, last = parts(u, c)

                def front(e, place):
                    at = (e, place)
                    m = n + 1
                    if at == (0, 1) and has_c:
                        dve.wait_ge(z_gained, m + 1)
                        dve.wait_ge(xb_ready, m + 1)
                        wait(dve, x1_kept_ready, m - 1)
                        dve.tensor_tensor(x1[(c + 1) % 2][:, :, :], z[:, :, :], xb[:, :, :], ALU.add).then_inc(x1_ready, 1)
                    if at == (0, 2) and has_c:
                        dve.wait_ge(x1_ready, m + 1)
                        token_stats(stat_c, x1[(c + 1) % 2], 0, NB // 2)
                    if at == (1, 1) and has_c:
                        token_stats(stat_c, x1[(c + 1) % 2], NB // 2, NB, stat_c_done)
                        norm_stats((stat_c, mean2_c, gap_c, ve_c),
                                   (stat_c_done, halves_c_done, terms_c_done, ve_c_done), m)
                    if at == (2, 0) and has_c:
                        norm_shift(shift_c, mean2_c, rstd_c, rstd_c_done, shift_c_done, m)
                        dve.wait_ge(shift_c_done, m + 1)
                        wait(dve, x1n_turned, m)
                        wait(dve, sum4_done, m)
                    pieces = {(2, 0): (0, 3), (2, 2): (3, 6), (3, 0): (6, NB)}.get(at)
                    if pieces and has_c:
                        for b in range(*pieces):
                            i = dve.tensor_scalar(x1n[:, b, :], x1[(c + 1) % 2][:, b, :], rstd_c[:, b:b + 1],
                                                  shift_c[:, b:b + 1], ALU.mult, ALU.add)
                        if pieces[1] == NB:
                            i.then_inc(x1n_ready, 1)
                    if at == (3, 1) and has_c:
                        dve.wait_ge(x_hi_ready, m + 1)
                        dve.tensor_tensor(x_lo[(c + 1) % 2][:, :], F[:, :], x_hi[(c + 1) % 2][:, :],
                                          ALU.subtract).then_inc(x_lo_ready, 1)
                    if at == (5, 0) and has_c:
                        dve.wait_ge(router_done, m + 1)
                        dve.tensor_tensor(logit[:, :], F[:, 0:NE], br_sb[:, :], ALU.add).then_inc(logit_ready, 1)
                        dve.wait_ge(logit_ready, m + 1)
                        dve.tensor_reduce(neg_top[:, :], logit[:, :], AX, ALU.max, negate=True
                                          ).then_inc(neg_top_done, 1)
                    if at == (5, 2) and has_c:
                        dve.wait_ge(ex_done, m + 1)
                        dve.reciprocal(ex_inv[:, :], ex_sum[:, :]).then_inc(ex_inv_done, 1)
                        dve.wait_ge(ex_inv_done, m + 1)
                        wait(dve, rw_turned, m)
                        dve.tensor_scalar(rw[:, :], ex[:, :], ex_inv[:, 0:1], None, ALU.mult).then_inc(rw_ready, 1)
                        dve.wait_ge(rw_ready, m + 1)
                        dve.tensor_copy(rw16[:, 0:NE], rw[:, :]).then_inc(rw_hi_ready, 1)
                        dve.wait_ge(rw_hi_ready, m + 1)
                        dve.tensor_tensor(rw16[:, NE:2 * NE], rw[:, :], rw16[:, 0:NE],
                                          ALU.subtract).then_inc(rw16_ready, 1)
                    m = n + 3
                    if at == (0, 0) and has_a:
                        wait(dve, xn_ready, m)
                        norm_shift(shift_a, mean2_a, rstd_a, rstd_a_done, shift_a_done, m)
                    if at == (4, 0) and has_a:
                        dve.wait_ge(xn_wa_ready, m + 1)
                        dve.tensor_reduce(factor[:, :], xn_wa[:, :, :], AX, ALU.add).then_inc(factor_sum_done, 1)
                        dve.wait_ge(factor_sum_done, m + 1)
                        dve.scalar_tensor_tensor(factor[:, :], factor[:, :], ALPHA, factor[:, :], ALU.mult,
                                                 ALU.max).then_inc(leaky_done, 1)
                    if at == (4, 2) and has_a:
                        dve.wait_ge(leaky_done, m + 1)
                        dve.wait_ge(adj_landed[(c + 3) % 2], 32 * (u + (c + 3) // 2 + 1))
                        dve.tensor_tensor(scores[:, :, :], adj_in[(c + 3) % 2][:, :, :], over_heads(factor, C),
                                          ALU.mult).then_inc(weighed, 1)
                        dve.wait_ge(weighed, m + 1)
                        dve.tensor_reduce(top[:, :], scores[:, :, :], AX, ALU.max).then_inc(top_done, 1)
                    if at == (5, 0) and has_a:
                        dve.wait_ge(top_done, m + 1)
                        dve.tensor_tensor(scores[:, :, :], scores[:, :, :], over_heads(top, C),
                                          ALU.subtract).then_inc(lowered, 1)
                    if at == (6, 1) and has_a:
                        dve.wait_ge(exp_done, m + 1)
                        dve.tensor_reduce(total[:, :], scores[:, :, :], AX, ALU.add).then_inc(total_done, 1)
                        dve.wait_ge(total_done, m + 1)
                        dve.reciprocal(inv_total[:, :], total[:, :]).then_inc(inv_total_done, 1)
                    if at == (6, 1) and has_a:
                        dve.wait_ge(inv_total_done, m + 1)
                        wait(dve, probs_turned, m - 1)
                        if isinstance(n, int) and n == -3:
                            dve.wait_ge(probs_zero, 2)
                        for k in range(2):
                            rows = slice(k * C, (k + 1) * C)
                            i = dve.tensor_tensor(probs[(c + 3) % 2][rows, :, k, :], scores[rows, :, :],
                                                  inv_total[rows, :].unsqueeze(2).broadcast_to([C, NB, C]), ALU.mult)
                        i.then_inc(probs_ready, 1)
                    m = n + 2
                    if at == (1, 2) and has_b:
                        leaky(mlp1, mlp1_linear, mlp1_ready, m)
                    if at == (3, 0) and has_b:
                        leaky(mlp2, mlp2_linear, mlp2_ready, m)
                    if at == (4, 1) and has_b:
                        dve.wait_ge(z_done, m + 1)
                        wait(dve, x1_ready, m)
                        dve.tensor_tensor(z[:, :, :], F[:, :].rearrange("p (b d) -> p b d", d=P),
                                          b3_wide[:, :].unsqueeze(1).broadcast_to([P, NB, P]), ALU.add
                                          ).then_inc(z_ready, 1)
                    if at == (5, 0) and has_b:
                        dve.wait_ge(z_ready, m + 1)
                        token_stats(stat_b, z, 0, NB // 2)
                    if at == (5, 1) and has_b:
                        token_stats(stat_b, z, NB // 2, NB, stat_b_done)
                        norm_stats((stat_b, mean2_b, gap_b, ve_b),
                                   (stat_b_done, halves_b_done, terms_b_done, ve_b_done), m)
                    if at == (6, 0) and has_b:
                        wait(dve, z_normed, m)
                        norm_shift(shift_b, mean2_b, rstd_b, rstd_b_done, shift_b_done, m)
                    if at == (1, 1) and last:
                        dve.wait_ge(y_done, NE * n)
                        dve.wait_ge(y_bias_ready, n)
                        dve.scalar_tensor_tensor(y_t[:, :].rearrange("p (b q) -> p b q", q=P),
                                                 Y[:, :].rearrange("p (b q) -> p b q", q=P), iuo_col[:, 0:1],
                                                 y_bias[:, :].unsqueeze(1).broadcast_to([P, NB, P]),
                                                 ALU.mult, ALU.add).then_inc(y_t_ready, 1)
                    if at == (2, 1) and last:
                        dve.wait_ge(y_turned, n)
                        dve.wait_ge(x1_kept_ready, n)
                        dve.wait_ge(y_out_free[(c - 1) % 2], 16 * (u + (c - 1) // 2 + 1))
                        dve.tensor_tensor(flat(y_out[(c - 1) % 2]), F[:, :], flat(x1_kept[(c - 1) % 2]),
                                          ALU.add).then_inc(y_out_ready, 1)
                    m = n + 4
                    if at == (6, 1) and has_next:
                        dve.wait_ge(x_landed[c % 2], 16 * (u + (c + 4) // 2 + 1))
                        token_stats(stat_a, x_in[c % 2], 0, NB // 2)
                    if at == (7, 0) and has_next:
                        token_stats(stat_a, x_in[c % 2], NB // 2, NB, stat_a_done)
                        norm_stats((stat_a, mean2_a, gap_a, ve_a),
                                   (stat_a_done, halves_a_done, terms_a_done, ve_a_done), m)

                for e in range(NE):
                    g = NE * n + e
                    k = (e - 1) % NE
                    step = (ffn and not (isinstance(g, int) and g == 0)) or (not ffn and last and e == 0)
                    front(e, 0)
                    if step:
                        dve.wait_ge(z2_done, g)
                        if isinstance(g, int) and g == 1:
                            dve.wait_ge(bias_ready, 1)
                        if k == 0:
                            dve.wait_ge(route_ready, n + 1)
                        Z = Z2[:, :].rearrange("p (b q) -> p b q", q=P)
                        par = (c - 1) % 2 if e == 0 else c % 2
                        wait(dve, h2_hi_ready, g - 1)
                        wait(dve, h2_lo_ready, g - 1)
                        dve.scalar_tensor_tensor(r2[:, :].rearrange("p (b q) -> p b q", q=P), Z, neg_bias2[:, k:k + 1],
                                                 route[par][:, k, :].unsqueeze(1).broadcast_to([P, NB, P]),
                                                 ALU.max, ALU.mult).then_inc(r2_ready, 1)
                    front(e, 1)
                    if step:
                        dve.wait_ge(h2_hi_ready, g)
                        wait(dve, y_done, g - 2)
                        dve.tensor_tensor(h2_lo[k % 2][:, :], r2[:, :], h2_hi[k % 2][:, :],
                                          ALU.subtract).then_inc(h2_lo_ready, 1)
                    front(e, 2)
                    if isinstance(n, int) and (n, e) in PREPARE:
                        prepare(PREPARE[n, e])
                if isinstance(n, int) and n == -4:
                    constants()

            pipeline(dve, body)

        @block.gpsimd
        def _(pool):
            pool.memset(ident[:, :], 0.0).then_inc(ident_zero, 1)
            pool.memset(same_e[:, :], 0.0).then_inc(same_zero, 1)
            pool.wait_ge(ident_zero, 1)
            pool.affine_select(out=ident[:, :], in_=ident[:, :], compare_op=ALU.not_equal, fill=1.0, base=0,
                               pattern=[[-1, P]], channel_multiplier=1).then_inc(ident_ready, 1)
            for t, value in ((ones, 1.0), (neg_half, -0.5)):
                i = pool.memset(t[:, :], value)
            i.then_inc(consts_ready, 1)
            pool.wait_ge(same_zero, 1)
            pool.memset(same_e[:, 0:NE * NE:NE + 1], 1.0).then_inc(same_ready, 1)
            for t in probs:
                pool.memset(t[:, :, :, :], 0.0).then_inc(probs_zero, 1)
            pool.wait_ge(consts_ready, 1)

            def rstd_of(ve, rstd, ve_done, rstd_done, m):
                pool.wait_ge(ve_done, m + 1)
                pool.tensor_tensor(rstd[:, :], ve[:, :], neg_half[:, 0:NB], ALU.pow).then_inc(rstd_done, 1)

            def prepare(step):
                if step == 0:
                    pool.wait_ge(bn_var, 1)
                    pool.tensor_tensor(v_col, v_col, neg_half[:, :].rearrange("p (l e) -> p l e", l=2), ALU.pow
                                       ).then_inc(bn_rstd, 1)
                layer = {2: 0, 4: 1, 5: 2}.get(step)
                if layer in (0, 1):
                    w = (e2_sb, eo_sb)[layer]
                    pool.wait_ge(iu_ready, layer + 1)
                    pool.wait_ge(abs_ready, layer + 2)
                    if layer == 1:
                        pool.wait_ge(c_done, 1)
                    pool.tensor_tensor(w[:, :, :], w[:, :, :], iu_col[:, layer, :].unsqueeze(2).broadcast_to([P, NE, P]),
                                       ALU.mult).then_inc(rows_scaled, 1)
                if layer is not None:
                    w, hi, lo = ((e1_sb, e1_hi, e1_lo), (e2_sb, e2_hi, e2_lo), (eo_sb, eo_hi, eo_lo))[layer]
                    pool.wait_ge(hi_ready, layer + 1)
                    pool.tensor_tensor(flat(lo), flat(w), flat(hi), ALU.subtract).then_inc(lo_ready, 1)

            def body(u, c):
                n, ffn, has_c, has_b, has_a, has_next, last = parts(u, c)

                def front(e):
                    m = n + 1
                    if e == 1 and has_c:
                        rstd_of(ve_c, rstd_c, ve_c_done, rstd_c_done, m)
                    if e == 2 and has_c:
                        pool.wait_ge(x1n_ready, m + 1)
                        pool.tensor_tensor(sum4[:, :, :], x1n[:, 0:4, :], x1n[:, 4:8, :], ALU.add).then_inc(sum4_done, 1)
                    if e == 3 and has_c:
                        pool.wait_ge(sum4_done, m + 1)
                        pool.tensor_tensor(sum2[:, :, :], sum4[:, 0:2, :], sum4[:, 2:4, :], ALU.add).then_inc(sum2_done, 1)
                        pool.wait_ge(sum2_done, m + 1)
                        wait(pool, feat_turned, m)
                        pool.tensor_tensor(feat[:, :], sum2[:, 0, :], sum2[:, 1, :], ALU.add).then_inc(feat_done, 1)
                    if e == 4 and has_c:
                        wait(pool, y_out_ready, m - 1)
                        pool.wait_ge(x1_ready, m + 1)
                        pool.tensor_tensor(x1_kept[(c + 1) % 2][:, :, :], x1[(c + 1) % 2][:, :, :],
                                           ones[:, :].unsqueeze(1).broadcast_to([P, NB, P]), ALU.mult
                                           ).then_inc(x1_kept_ready, 1)
                    m = n + 3
                    if e == 2 and has_a:
                        pool.wait_ge(xn_ready, m + 1)
                        wait(pool, factor_sum_done, m)
                        pool.tensor_tensor(xn_wa[:, :, :], xn[(c + 3) % 2][:, :, :],
                                           wa_wide[:, :].unsqueeze(1).broadcast_to([P, NB, P]), ALU.mult
                                           ).then_inc(xn_wa_ready, 1)
                    m = n + 2
                    if e == 3 and has_b:
                        pool.wait_ge(x_landed[c % 2], 16 * (u + (c + 2) // 2 + 1))
                        if isinstance(n, int) and n == -2:
                            pool.wait_ge(gnn_landed, 16 * len(GNN_LOADS))
                        wait(pool, x1_ready, m)
                        pool.tensor_tensor(xb[:, :, :], x_in[c % 2][:, :, :],
                                           lnb[:, :].unsqueeze(1).broadcast_to([P, NB, P]), ALU.add
                                           ).then_inc(xb_ready, 1)
                    if e == 5 and has_b:
                        wait(pool, z_normed, m)
                        rstd_of(ve_b, rstd_b, ve_b_done, rstd_b_done, m)
                    m = n + 4
                    if e == 7 and has_next:
                        wait(pool, xn_ready, m)
                        rstd_of(ve_a, rstd_a, ve_a_done, rstd_a_done, m)
                    m = n + 2
                    if e == 7 and has_b:
                        pool.wait_ge(z_normed, m + 1)
                        pool.tensor_tensor(z[:, :, :], z[:, :, :], lng[:, :].unsqueeze(1).broadcast_to([P, NB, P]),
                                           ALU.mult).then_inc(z_gained, 1)

                for e in range(NE):
                    g = NE * n + e
                    if ffn:
                        pool.wait_ge(h1_hi_ready, g + 1)
                        wait(pool, z2_done, g - 1)
                        pool.tensor_tensor(h1_lo[e % 2][:, :], r1[e % 2][:, :], h1_hi[e % 2][:, :],
                                           ALU.subtract).then_inc(h1_lo_ready, 1)
                    front(e)
                    if isinstance(n, int) and (n, e) in PREPARE:
                        prepare(PREPARE[n, e])

            pipeline(pool, body)


NAMES = ("x", "adj", *("L0_gnn_" + k for k in ("W", "a", "ln_g", "ln_b", "W1", "b1", "W2", "b2", "W3", "b3")),
         *("L0_ffn_" + k for k in ("Wr", "br", "W1", "b1", "g1", "be1", "m1", "v1", "W2", "b2", "g2", "be2", "m2",
                                   "v2", "Wo", "bo")))


def kernel(**inputs):
    import numpy as _np
    import concourse.bacc as _bacc
    from concourse import mybir as _mybir
    from concourse.bass_utils import run_bass_kernel_spmd as _run

    nc = _bacc.Bacc("TRN2", target_bir_lowering=False, num_devices=1)
    arrays, args = {}, []
    for name in NAMES:
        a = _np.ascontiguousarray(inputs[name])
        arrays[f"in_{name}_dram"] = a
        args.append(nc.dram_tensor(f"in_{name}_dram", a.shape, _mybir.dt.from_np(a.dtype), kind="ExternalInput").ap())
    args.append(nc.dram_tensor("out_0_dram", inputs["x"].shape, _mybir.dt.float32, kind="ExternalOutput").ap())
    build(nc, *args)
    return _run(nc, [arrays], core_ids=[0]).results[0]["out_0_dram"]
```
